# Optimizing a Trainium2 kernel written in Bass

```python
import numpy as np
import jax
import jax.numpy as jnp

def _softmax(x, axis=-1):
    return jax.nn.softmax(x, axis=axis)

def _gelu(x):
    return jax.nn.gelu(x, approximate=True)

def _silu(x):
    return jax.nn.silu(x)

def _sigmoid(x):
    return jax.nn.sigmoid(x)

def _layernorm(x, axis=-1, eps=1e-05):
    m = jnp.mean(x, axis=axis, keepdims=True)
    v = jnp.var(x, axis=axis, keepdims=True)
    return (x - m) / jnp.sqrt(v + eps)

def _scatter_add(tgt, idx, src, axis=0):
    return tgt.at[idx].add(src)

def _segment_sum(src, seg, n):
    return jax.ops.segment_sum(src, seg, n)
kernel_name = 'mk_adj_resnorm_d4_adj_r2_af7c5c'

def setup_inputs(seed: int=0):
    np.random.seed(seed)
    _w = jnp.asarray

    def _rec_inputs():
        import jax
        import jax.numpy as jnp
        _gk = jax.random.key(seed)
        x = -0.006082 + 1.001 * jax.random.normal(jax.random.fold_in(_gk, 1), (4096, 64), jnp.float32)
        _w = (1.0 + jnp.arange(4096, dtype=jnp.float32)) ** (-0.5)
        _w = _w / _w.mean()
        _pij = jnp.clip(0.000976562 * _w[:, None] * _w[None, :], 0.0, 1.0)
        _a = jax.random.uniform(jax.random.fold_in(_gk, 2), (4096, 4096)) < _pij
        adj = _a.astype(jnp.int32)
        return (x, adj)
    x, adj = _rec_inputs()

    def _L0_gnn_setup():
        import jax, jax.numpy as jnp
        import numpy as np
        ALPHA = 0.2
        NEG_INF = -9000000000000000.0
        key = jax.random.key(seed)
        k1, k2, k3, k4 = jax.random.split(key, 4)
        N, F_IN, F_OUT = (512, 64, 64)
        h = jax.random.normal(k1, (N, F_IN), dtype=jnp.float32)
        adj = jax.random.randint(k2, (N, N), 0, 2, dtype=jnp.int32)
        lim_W = 1.414 * np.sqrt(6.0 / (F_IN + F_OUT))
        W = jax.random.uniform(k3, (F_IN, F_OUT), minval=-lim_W, maxval=lim_W, dtype=jnp.float32)
        lim_a = 1.414 * np.sqrt(6.0 / (2 * F_OUT + 1))
        a = jax.random.uniform(k4, (2 * F_OUT, 1), minval=-lim_a, maxval=lim_a, dtype=jnp.float32)
        return {'h': h, 'adj': adj, 'W': W, 'a': a}
    _L0_gnn_all = _L0_gnn_setup()
    _L0_gnn_in = {k: v for k, v in _L0_gnn_all.items() if k in ('W', 'a')}
    del _L0_gnn_all

    def _L1_gnn_setup():
        import jax, jax.numpy as jnp
        import numpy as np
        N = 4096
        F_IN = 64
        F_OUT = 64
        NEG_SLOPE = 0.01
        MASK_FILL = -1000000000000.0
        key = jax.random.key(seed)
        k1, k2, k3, k4 = jax.random.split(key, 4)
        x = jax.random.normal(k1, (N, F_IN), dtype=jnp.float32)
        adj_matrix = jax.random.randint(k2, (N, N), 0, 2, dtype=jnp.int32)
        W = jax.random.normal(k3, (F_IN, F_OUT), dtype=jnp.float32) * (1.0 / np.sqrt(F_IN))
        a = jax.random.normal(k4, (2 * F_IN, 1), dtype=jnp.float32) * (1.0 / np.sqrt(2 * F_IN))
        return {'x': x, 'adj_matrix': adj_matrix, 'W': W, 'a': a}
    _L1_gnn_all = _L1_gnn_setup()
    _L1_gnn_in = {k: v for k, v in _L1_gnn_all.items() if k in ('W', 'a')}
    del _L1_gnn_all

    def _L2_gnn_setup():
        import jax, jax.numpy as jnp
        import numpy as np
        N = 4096
        D = 64
        NEG_INF = -9000000000000000.0
        LEAKY_SLOPE = 0.01
        key = jax.random.key(seed)
        k1, k2, k3 = jax.random.split(key, 3)
        h = jax.random.normal(k1, (N, D), dtype=jnp.float32)
        adj = jax.random.randint(k2, (N, N), 0, 2, dtype=jnp.int32)
        bound = float(np.sqrt(6.0 / (2 * D + 1)))
        a = jax.random.uniform(k3, (2 * D, 1), dtype=jnp.float32, minval=-bound, maxval=bound)
        return {'h': h, 'adj': adj, 'a': a}
    _L2_gnn_all = _L2_gnn_setup()
    _L2_gnn_in = {k: v for k, v in _L2_gnn_all.items() if k in ('a',)}
    del _L2_gnn_all

    def _L3_gnn_setup():
        import jax, jax.numpy as jnp
        import numpy as np
        ALPHA = 0.2
        NEG_BIG = jnp.float32(-9000000000000000.0)
        key = jax.random.key(seed)
        k1, k2, k3, k4 = jax.random.split(key, 4)
        N, F_IN, F_OUT = (4096, 64, 64)
        inputs = jax.random.normal(k1, (N, F_IN), dtype=jnp.float32)
        adj = jax.random.randint(k2, (N, N), 0, 2, dtype=jnp.int32)
        gain = 1.414
        lim_w = gain * np.sqrt(6.0 / (F_IN + F_OUT))
        W = jax.random.uniform(k3, (F_IN, F_OUT), dtype=jnp.float32, minval=-lim_w, maxval=lim_w)
        lim_a = gain * np.sqrt(6.0 / (2 * F_OUT + 1))
        a = jax.random.uniform(k4, (2 * F_OUT, 1), dtype=jnp.float32, minval=-lim_a, maxval=lim_a)
        return {'inputs': inputs, 'adj': adj, 'W': W, 'a': a}
    _L3_gnn_all = _L3_gnn_setup()
    _L3_gnn_in = {k: v for k, v in _L3_gnn_all.items() if k in ('W', 'a')}
    del _L3_gnn_all
    return {'x': x, 'adj': adj, 'L0_gnn_W': _L0_gnn_in['W'], 'L0_gnn_a': _L0_gnn_in['a'], 'L1_gnn_W': _L1_gnn_in['W'], 'L1_gnn_a': _L1_gnn_in['a'], 'L2_gnn_a': _L2_gnn_in['a'], 'L3_gnn_W': _L3_gnn_in['W'], 'L3_gnn_a': _L3_gnn_in['a']}

def reference(x, adj, L0_gnn_W, L0_gnn_a, L1_gnn_W, L1_gnn_a, L2_gnn_a, L3_gnn_W, L3_gnn_a):
    import jax
    import jax.numpy as jnp

    def _L0_gnn_ref(h, adj, W, a):
        import jax, jax.numpy as jnp
        import numpy as np
        ALPHA = 0.2
        NEG_INF = -9000000000000000.0
        F_OUT = W.shape[1]
        Wh = h @ W
        a1, a2 = (a[:F_OUT, 0], a[F_OUT:, 0])
        e = (Wh @ a1)[:, None] + (Wh @ a2)[None, :]
        e = jax.nn.leaky_relu(e, negative_slope=ALPHA)
        scores = jnp.where(adj > 0, e, jnp.float32(NEG_INF))
        attention = jax.nn.softmax(scores, axis=1)
        h_prime = attention @ Wh
        return jax.nn.elu(h_prime)

    def _L1_gnn_ref(x, adj_matrix, W, a):
        import jax, jax.numpy as jnp
        import numpy as np
        N = 4096
        F_IN = 64
        F_OUT = 64
        NEG_SLOPE = 0.01
        MASK_FILL = -1000000000000.0
        h = x @ W
        a1 = a[:F_OUT, 0]
        a2 = a[F_OUT:, 0]
        f1 = h @ a1
        f2 = h @ a2
        e = jax.nn.leaky_relu(f1[:, None] + f2[None, :], NEG_SLOPE)
        e = jnp.where(adj_matrix > 0, e, MASK_FILL)
        attention = jax.nn.softmax(e, axis=1)
        h_prime = attention @ h
        return jax.nn.elu(h_prime)

    def _L2_gnn_ref(h, adj, a):
        import jax, jax.numpy as jnp
        import numpy as np
        N = 4096
        D = 64
        NEG_INF = -9000000000000000.0
        LEAKY_SLOPE = 0.01
        a1 = a[:D, 0]
        a2 = a[D:, 0]
        src = h @ a1
        dst = h @ a2
        e = src[:, None] + dst[None, :]
        e = jnp.where(e > 0, e, LEAKY_SLOPE * e)
        e = jnp.where(adj > 0, e, NEG_INF)
        attention = jax.nn.softmax(e, axis=1)
        h_prime = attention @ h
        return h_prime

    def _L3_gnn_ref(inputs, adj, W, a):
        import jax, jax.numpy as jnp
        import numpy as np
        ALPHA = 0.2
        NEG_BIG = jnp.float32(-9000000000000000.0)
        Wh = inputs @ W
        F_out = W.shape[1]
        a_src = a[:F_out, 0]
        a_dst = a[F_out:, 0]
        e = (Wh @ a_src)[:, None] + (Wh @ a_dst)[None, :]
        e = jnp.where(e > 0, e, ALPHA * e)
        scores = jnp.where(adj > 0, e, NEG_BIG)
        attention = jax.nn.softmax(scores, axis=1)
        h_prime = attention @ Wh
        return jax.nn.elu(h_prime)
    x = _layernorm(x + _L0_gnn_ref(x, adj, L0_gnn_W, L0_gnn_a), axis=-1)
    x = _layernorm(x + _L1_gnn_ref(x, adj, L1_gnn_W, L1_gnn_a), axis=-1)
    x = _layernorm(x + _L2_gnn_ref(x, adj, L2_gnn_a), axis=-1)
    x = _layernorm(x + _L3_gnn_ref(x, adj, L3_gnn_W, L3_gnn_a), axis=-1)
    return x

_drawn_inputs = setup_inputs


def setup_inputs(seed=0):
    import zlib

    import numpy as np

    out = dict(_drawn_inputs(seed))
    spreads = {}
    factors = {}
    for name, (base, spread) in spreads.items():
        noise = np.random.default_rng([zlib.crc32(name.encode()), seed]).standard_normal(out[name].shape)
        drawn = base * np.exp(spread * noise) if base else spread * noise
        out[name] = jnp.asarray(drawn.astype(out[name].dtype))
    for name, factor in factors.items():
        out[name] = (out[name] * factor).astype(out[name].dtype)
    return out
```

```python
from contextlib import ExitStack

import concourse.bass as bass
from concourse import mybir
from concourse.alu_op_type import AluOpType as ALU

ACT = mybir.ActivationFunctionType
AX_X = mybir.AxisListType.X
F32 = mybir.dt.float32
F16 = mybir.dt.float16
FP8 = mybir.dt.float8e4
U8 = mybir.dt.uint8
I32 = mybir.dt.int32
RMAX = bass.bass_isa.ReduceOp.max

P = 128
N = 4096
D = 64
L = 4
NB = N // P
G = 8
GB = NB // G
GN = N // G
SLOPES = (0.2, 0.01, 0.01, 0.2)
HAS_ELU = (1.0, 1.0, 0.0, 1.0)
EPS = 1e-5
EDGE = 2.0
EDGE_BYTE = 64.0
S_COL, D_COL, H_COL = 0, 1, 2
PW = H_COL + D
EPI = 11


class Bag:
    pass


def place(nc, ctx):
    m = Bag()

    def sb(name, shape, dt):
        return ctx.enter_context(nc.sbuf_tensor(name, shape, dt))

    m.mask = sb("mask", [P, G, NB, GN], FP8)
    m.x = sb("x", [P, NB, D], F32)
    m.stage = sb("stage", [P, 6, GN], I32)
    m.proj = sb("proj", [P, NB, PW + 1], F32)
    m.xT = sb("xT", [D, GN], F32)
    m.vals = sb("vals", [P, NB * 4 * (D + 1)], F16)
    m.srow = sb("srow", [P, G, GN], F32)
    m.edges = sb("edges", [P, 8, GN], FP8)
    m.nd = sb("nd", [P, GB, D + 1], F32)
    m.t0 = sb("t0", [P, GB, D + 1], F32)
    m.t1 = sb("t1", [P, GB, D], F32)
    m.t2 = sb("t2", [P, GB, D], F32)
    m.small = sb("small", [P, 12, GB], F32)
    m.halfneg = sb("halfneg", [P, GB], F32)
    m.ident = sb("ident", [P, P], F32)
    m.ones = sb("ones", [P, P], F32)
    m.wall = sb("wall", [D, L, PW], F32)
    m.wT = sb("wT", [D, 3, D], F32)
    m.avec = sb("avec", [D, L, 2], F32)
    m.par = sb("par", [P, L, 2], F32)
    m.wcur = sb("wcur", [D, PW], F32)
    m.pcur = sb("pcur", [P, 2], F32)
    m.hsum = sb("hsum", [P, D + 1], F32)
    m.ps = ctx.enter_context(nc.psum_tensor("ps", [P, 8, 512], F32))
    return m


def wait(eng, sem, value):
    eng.wait_ge(sem, value)
    if not isinstance(value, int):
        eng.nop(nofuse=True)



def general(nc, m, out):
    with ExitStack() as ctx:
        def sem(name):
            return ctx.enter_context(nc.semaphore("g_" + name))

        par_ready = sem("par_ready")
        xT_in_psum = sem("xT_in_psum")
        xT_ready = sem("xT_ready")
        proj_in_psum = sem("proj_in_psum")
        proj_ready = sem("proj_ready")
        hsum_in_psum = sem("hsum_in_psum")
        hsum_ready = sem("hsum_ready")
        dneg_ready = sem("dneg_ready")
        dmin_ready = sem("dmin_ready")
        dve_step = sem("dve_step")
        acc_step = sem("acc_step")
        accT_in_psum = sem("accT_in_psum")
        chain = sem("chain")
        rows_in_psum = sem("rows_in_psum")
        rows_ready = sem("rows_ready")
        low_ready = sem("low_ready")
        score_ready = sem("score_ready")
        exp_ready = sem("exp_ready")
        prob_ready = sem("prob_ready")
        prob_used = sem("prob_used")
        epi = epilogue_semaphores(sem)
        out_done = sem("out_done")

        f = m.vals[:].bitcast(F32)

        def region(k, n=1):
            return f[:, k * GN:(k + n) * GN]

        acc = region(0)
        rows = region(1, 2).rearrange("p (r i) -> p r i", r=2)
        score = region(3, 2).rearrange("p (r i) -> p r i", r=2)
        prob = region(5, 2).rearrange("p (r i) -> p r i", r=2)
        diag = m.srow[:, 0:2, :]
        cols = m.srow[:, 2, :]
        dshift = cols[:, 0:NB]
        dslope = cols[:, NB:2 * NB]
        dneg = cols[:, 2 * NB:3 * NB]
        dnegmax = cols[:, 3 * NB:3 * NB + 1]
        dmin_neg = cols[:, 3 * NB + 1:3 * NB + 2]
        mu, q, top, r1, r2, q2 = (cols[:, 4 * NB + GB * k:4 * NB + GB * (k + 1)] for k in range(6))
        mask8 = m.mask[:].bitcast(U8)
        slope = m.pcur[:, 0:1]
        scol = m.proj[:, :, S_COL]
        dcol = m.proj[:, :, D_COL]
        block = ctx.enter_context(nc.Block())

        @block.tensor
        def _(pe):
            with pe.Fori(0, L) as l:
                wait(pe, par_ready, l + 1)
                wait(pe, epi.x_ready, l * G + 1)
                for c in range(G):
                    if c >= 1:
                        wait(pe, xT_ready, l * G + c)
                    for b in range(GB):
                        last = nc.tensor.transpose(m.ps[0:D, 0, b * P:(b + 1) * P], m.x[:, c * GB + b, :], m.ident[:])
                    last.then_inc(xT_in_psum, 1)
                    wait(pe, xT_ready, l * G + c + 1)
                    if c >= 1:
                        wait(pe, proj_ready, l * G + c)
                    for b in range(GB):
                        last = nc.tensor.matmul(m.ps[:, 1, b * PW:(b + 1) * PW], m.xT[:, b * P:(b + 1) * P], m.wcur[:],
                                                start=b == 0, stop=b == GB - 1, skip_group_check=True)
                    last.then_inc(proj_in_psum, 1)
                wait(pe, proj_ready, l * G + G)
                for b in range(NB):
                    last = nc.tensor.matmul(m.ps[:, 2, 0:D + 1], m.ones[:], m.proj[:, b, H_COL:],
                                            start=b == 0, stop=b == NB - 1)
                last.then_inc(hsum_in_psum, 1)
                with pe.Fori(0, G) as g:
                    k = l * G + g
                    wait(pe, acc_step, k * NB + NB)
                    for b in range(GB):
                        last = nc.tensor.transpose(m.ps[:, 3, b * P:(b + 1) * P], acc[:, b * P:(b + 1) * P], m.ident[:])
                    last.then_inc(accT_in_psum, 1)
                    wait(pe, chain, k * 7 + 7)
                    for r in range(2):
                        last = nc.tensor.matmul(m.ps[:, 4 + r, :], m.ones[:], diag[:, r, :], start=True, stop=True)
                    last.then_inc(rows_in_psum, 1)

                    def products(t, first):
                        for u in range(2):
                            wait(pe, prob_ready, k * NB + t + u + 1)
                            for b in range(GB):
                                last = nc.tensor.matmul(
                                    m.ps[:, 6, b * (D + 1):(b + 1) * (D + 1)], prob[:, u, b * P:(b + 1) * P],
                                    m.proj[:, bass.ds(t + u, 1), H_COL:].rearrange("p a n -> p (a n)"),
                                    start=first and u == 0 and b == 0, stop=False, skip_group_check=True)
                            last.then_inc(prob_used, 1)

                    products(0, True)
                    with pe.Fori(1, NB // 2) as pair:
                        products(2 * pair, False)

        @block.scalar
        def _(act):
            with act.Fori(0, L) as l:
                for c in range(G):
                    wait(act, xT_in_psum, l * G + c + 1)
                    if c >= 1:
                        wait(act, proj_in_psum, l * G + c)
                    nc.scalar.copy(m.xT[:], m.ps[0:D, 0, :]).then_inc(xT_ready, 1)
                    wait(act, proj_in_psum, l * G + c + 1)
                    nc.scalar.copy(m.proj[:, c * GB:(c + 1) * GB, 0:PW],
                                   m.ps[:, 1, 0:GB * PW].rearrange("p (b n) -> p b n", b=GB)).then_inc(proj_ready, 1)
                wait(act, hsum_in_psum, l + 1)
                nc.scalar.copy(m.hsum[:], m.ps[:, 2, 0:D + 1]).then_inc(hsum_ready, 1)
                wait(act, dve_step, l * 3 + 3)
                with act.Fori(0, G) as g:
                    k = l * G + g
                    wait(act, rows_in_psum, k + 1)
                    nc.scalar.copy(rows, m.ps[:, 4:6, :]).then_inc(rows_ready, 1)
                    wait(act, rows_ready, k + 1)
                    with act.Fori(0, NB // 2) as pair:
                        t = 2 * pair
                        for u in range(2):
                            n = k * NB + t + u
                            nc.scalar.activation(score[:, u, :], rows[:, 1, :], ACT.Identity,
                                                 bias=dslope[:, bass.ds(t + u, 1)]).then_inc(low_ready, 1)
                        for u in range(2):
                            n = k * NB + t + u
                            wait(act, score_ready, n + 1)
                            nc.scalar.activation(prob[:, u, :], score[:, u, :], ACT.Exp).then_inc(exp_ready, 1)
                        wait(act, exp_ready, k * NB + t + 2)
                        wait(act, prob_used, k * NB + t + 2)
                    wait(act, epi.x_ready, k + 1)
                    nc.scalar.copy(m.nd[:], m.ps[:, 6, 0:GB * (D + 1)].rearrange("p (b n) -> p b n", b=GB)
                                   ).then_inc(epi.nd_ready, 1)
                    epilogue_act(nc, act, m, epi, k)

        @block.vector
        def _(dve):
            with dve.Fori(0, L) as l:
                nc.vector.tensor_copy(m.wcur[:], m.wall[:, bass.ds(l, 1), :].rearrange("p a n -> p (a n)"))
                nc.vector.tensor_copy(m.pcur[:], m.par[:, bass.ds(l, 1), :].rearrange("p a n -> p (a n)")
                                      ).then_inc(par_ready, 1)
                wait(dve, par_ready, l + 1)
                wait(dve, proj_ready, l * G + G)
                nc.vector.tensor_scalar(dneg, dcol, -1.0, None, ALU.mult).then_inc(dve_step, 1)
                nc.vector.tensor_scalar(dslope, dcol, slope, None, ALU.mult)
                wait(dve, dve_step, l * 3 + 1)
                nc.vector.tensor_reduce(dnegmax, dneg, op=ALU.max, axis=AX_X).then_inc(dve_step, 1)
                wait(dve, dmin_ready, l + 1)
                nc.vector.tensor_scalar(dshift, dcol, dmin_neg, 1.0, ALU.add, ALU.add).then_inc(dve_step, 1)
                wait(dve, dve_step, l * 3 + 3)
                with dve.Fori(0, G) as g:
                    k = l * G + g
                    nc.vector.memset(acc, 0.0).then_inc(chain, 1)
                    wait(dve, chain, k * 7 + 1)
                    with dve.Fori(0, NB) as t:
                        nc.vector.scalar_tensor_tensor(
                            acc, mask8[:, bass.ds(g, 1), bass.ds(t, 1), :].rearrange("p a b n -> p (a b n)"),
                            dshift[:, bass.ds(t, 1)], acc, ALU.mult, ALU.max).then_inc(acc_step, 1)
                        wait(dve, acc_step, k * NB + t + 1)
                    wait(dve, accT_in_psum, k + 1)
                    nc.vector.tensor_reduce(mu, m.ps[:, 3, :].rearrange("p (b n) -> p b n", b=GB),
                                            op=ALU.max, axis=AX_X).then_inc(chain, 1)
                    wait(dve, chain, k * 7 + 2)
                    nc.vector.tensor_scalar(q2, mu, 1.0 / EDGE_BYTE, dmin_neg, ALU.mult, ALU.subtract
                                            ).then_inc(chain, 1)
                    wait(dve, chain, k * 7 + 3)
                    nc.vector.scalar_tensor_tensor(q, q2, -1.0, scol[:, bass.ds(g * GB, GB)], ALU.add, ALU.add
                                                   ).then_inc(chain, 1)
                    wait(dve, chain, k * 7 + 4)
                    nc.vector.scalar_tensor_tensor(top, q, slope, q, ALU.mult, ALU.max).then_inc(chain, 1)
                    wait(dve, chain, k * 7 + 5)
                    nc.vector.tensor_tensor(r1, scol[:, bass.ds(g * GB, GB)], top, ALU.subtract)
                    nc.vector.scalar_tensor_tensor(r2, scol[:, bass.ds(g * GB, GB)], slope, top, ALU.mult,
                                                   ALU.subtract).then_inc(chain, 1)
                    wait(dve, chain, k * 7 + 6)
                    for r, col in enumerate((r1, r2)):
                        for b in range(GB):
                            last = nc.vector.tensor_scalar(diag[:, r, b * P:(b + 1) * P], m.ident[:], col[:, b:b + 1],
                                                           None, ALU.mult)
                    last.then_inc(chain, 1)
                    wait(dve, rows_ready, k + 1)
                    with dve.Fori(0, NB // 2) as pair:
                        t = 2 * pair
                        for u in range(2):
                            n = k * NB + t + u
                            wait(dve, low_ready, n + 1)
                            nc.vector.scalar_tensor_tensor(score[:, u, :], rows[:, 0, :], dcol[:, bass.ds(t + u, 1)],
                                                           score[:, u, :], ALU.add, ALU.max).then_inc(score_ready, 1)
                        for u in range(2):
                            n = k * NB + t + u
                            wait(dve, exp_ready, n + 1)
                            nc.vector.scalar_tensor_tensor(
                                prob[:, u, :],
                                mask8[:, bass.ds(g, 1), bass.ds(t + u, 1), :].rearrange("p a b n -> p (a b n)"),
                                3.2e38 / EDGE_BYTE, prob[:, u, :], ALU.mult, ALU.min).then_inc(prob_ready, 1)
                    epilogue_dve(nc, dve, m, epi, k)

        @block.gpsimd
        def _(pool):
            nc.gpsimd.sem_inc(epi.x_ready, 1)
            with pool.Fori(0, L) as l:
                wait(pool, dve_step, l * 3 + 2)
                nc.gpsimd.partition_all_reduce(dmin_neg, dnegmax, P, RMAX).then_inc(dmin_ready, 1)
                wait(pool, hsum_ready, l + 1)
                with pool.Fori(0, G) as g:
                    k = l * G + g
                    epilogue_pool(nc, pool, m, epi, k, m.x[:, bass.ds(g * GB, GB), :])

        @block.sync
        def _(sp):
            wait(sp, epi.x_ready, L * G + 1)
            sp.dma_start(out.rearrange("(b p) f -> p b f", p=P), m.x[:]).then_inc(out_done, 16)
            wait(sp, out_done, 16)



def epilogue_semaphores(sem):
    e = Bag()
    e.nd_ready = sem("nd_ready")
    e.pool_step = sem("pool_step")
    e.recip_ready = sem("recip_ready")
    e.exp_min = sem("exp_min")
    e.elu_step = sem("elu_step")
    e.sum_ready = sem("sum_ready")
    e.var_ready = sem("var_ready")
    e.x_ready = sem("x_ready")
    return e


def epilogue_pool(nc, pool, m, e, k, x):
    s = m.small
    zero, recip, total, negmean, sqsum, var, rstd = (s[:, n, :] for n in range(7))

    def wide(v):
        return v.unsqueeze(2).to_broadcast([P, GB, D])

    step = k * EPI
    wait(pool, e.nd_ready, k + 1)
    nc.gpsimd.tensor_scalar(zero, m.nd[:, :, D], 0.0, None, ALU.is_equal).then_inc(e.pool_step, 1)
    wait(pool, e.pool_step, step + 1)
    nc.gpsimd.tensor_tensor(m.t0[:], zero.unsqueeze(2).to_broadcast([P, GB, D + 1]),
                            m.hsum[:].unsqueeze(1).to_broadcast([P, GB, D + 1]), ALU.mult).then_inc(e.pool_step, 1)
    wait(pool, e.pool_step, step + 2)
    nc.gpsimd.tensor_tensor(m.nd[:], m.nd[:], m.t0[:], ALU.add).then_inc(e.pool_step, 1)
    wait(pool, e.recip_ready, k + 1)
    h = m.t0[:, :, 0:D]
    nc.gpsimd.tensor_tensor(h, m.nd[:, :, 0:D], wide(recip), ALU.mult).then_inc(e.pool_step, 1)
    wait(pool, e.pool_step, step + 4)
    nc.gpsimd.tensor_scalar(m.t1[:], h, 0.0, None, ALU.min).then_inc(e.pool_step, 1)
    y = m.nd[:, :, 0:D]
    nc.gpsimd.tensor_tensor(y, x, h, ALU.add).then_inc(e.pool_step, 1)
    wait(pool, e.sum_ready, k + 1)
    nc.gpsimd.tensor_scalar(negmean, total, -1.0 / D, 0.0, ALU.mult, ALU.add).then_inc(e.pool_step, 1)
    wait(pool, e.pool_step, step + 7)
    nc.gpsimd.tensor_tensor(m.t1[:], y, wide(negmean), ALU.add).then_inc(e.pool_step, 1)
    wait(pool, e.var_ready, k + 1)
    nc.gpsimd.tensor_scalar(var, sqsum, 1.0 / D, EPS, ALU.mult, ALU.add).then_inc(e.pool_step, 1)
    wait(pool, e.pool_step, step + 9)
    nc.gpsimd.tensor_tensor(rstd, var, m.halfneg[:], ALU.pow).then_inc(e.pool_step, 1)
    wait(pool, e.pool_step, step + 10)
    nc.gpsimd.tensor_tensor(x, m.t1[:], wide(rstd), ALU.mult).then_inc(e.pool_step, 1)
    wait(pool, e.pool_step, step + 11)
    nc.gpsimd.sem_inc(e.x_ready, 1)


def epilogue_act(nc, act, m, e, k):
    s = m.small
    zero, recip, total, negmean, sqsum, var, rstd = (s[:, n, :] for n in range(7))
    y = m.nd[:, :, 0:D]
    wait(act, e.pool_step, k * EPI + 5)
    nc.scalar.activation(m.t2[:], m.t1[:], ACT.Exp).then_inc(e.exp_min, 1)
    wait(act, e.elu_step, k * 2 + 2)
    for b in range(GB):
        last = nc.scalar.activation(m.t2[:, b, :], y[:, b, :], ACT.Identity, accum_out=total[:, b:b + 1])
    last.then_inc(e.sum_ready, 1)
    wait(act, e.pool_step, k * EPI + 7)
    wait(act, e.sum_ready, k + 1)
    for b in range(GB):
        last = nc.scalar.activation(m.t2[:, b, :], y[:, b, :], ACT.Square, bias=negmean[:, b:b + 1],
                                    accum_out=sqsum[:, b:b + 1])
    last.then_inc(e.var_ready, 1)


def epilogue_dve(nc, dve, m, e, k):
    recip = m.small[:, 1, :]
    y = m.nd[:, :, 0:D]
    wait(dve, e.pool_step, k * EPI + 3)
    nc.vector.reciprocal(recip, m.nd[:, :, D]).then_inc(e.recip_ready, 1)
    wait(dve, e.exp_min, k + 1)
    wait(dve, e.pool_step, k * EPI + 6)
    nc.vector.scalar_tensor_tensor(m.t1[:], m.t2[:], -1.0, m.t1[:], ALU.add, ALU.subtract).then_inc(e.elu_step, 1)
    wait(dve, e.elu_step, k * 2 + 1)
    nc.vector.scalar_tensor_tensor(y, m.t1[:], m.pcur[:, 1:2], y, ALU.mult, ALU.add).then_inc(e.elu_step, 1)
    wait(dve, e.elu_step, k * 2 + 2)



def load(nc, m, x, adjT, ws, wTs, avecs):
    with ExitStack() as ctx:
        def sem(name):
            return ctx.enter_context(nc.semaphore("l_" + name))

        x_loaded = sem("x_loaded")
        w_loaded = sem("w_loaded")
        zeroed = sem("zeroed")
        ident_ready = sem("ident_ready")
        wa_in_psum = sem("wa_in_psum")
        wa_ready = sem("wa_ready")
        adj_loaded = [sem(f"adj_loaded{n}") for n in range(6)]
        masked = sem("masked")
        block = ctx.enter_context(nc.Block())
        adj_v = adjT.rearrange("(t p) (g i) -> p g t i", p=P, g=G)

        @block.sync
        def _(sp):
            sp.dma_start(m.x[:], x.rearrange("(b p) f -> p b f", p=P)).then_inc(x_loaded, 16)
            for n in range(3):
                l = (0, 1, 3)[n]
                sp.dma_start(m.wall[:, l, H_COL:], ws[n]).then_inc(w_loaded, 16)
                sp.dma_start(m.wT[:, n, :], wTs[n]).then_inc(w_loaded, 16)
            for l in range(L):
                sp.dma_start(m.avec[:, l, :], avecs[l]).then_inc(w_loaded, 16)
            for n in range(G * NB):
                if n >= 6:
                    sp.wait_ge(masked, n - 5)
                    sp.wait_ge(adj_loaded[n % 6], 16 * (n // 6))
                sp.dma_start(m.stage[:, n % 6, :], adj_v[:, n // NB, n % NB, :]).then_inc(adj_loaded[n % 6], 16)
            sp.wait_ge(x_loaded, 16)

        @block.gpsimd
        def _(pool):
            nc.gpsimd.memset(m.ident[:], 0.0).then_inc(zeroed, 1)
            pool.wait_ge(zeroed, 1)
            nc.gpsimd.affine_select(out=m.ident[:], in_=m.ident[:], compare_op=ALU.not_equal, fill=1.0, base=0,
                                    pattern=[[-1, P]], channel_multiplier=1).then_inc(ident_ready, 1)

        @block.vector
        def _(dve):
            nc.vector.memset(m.ones[:], 1.0)
            nc.vector.memset(m.halfneg[:], -0.5)
            nc.vector.memset(m.proj[:, :, PW], 1.0)
            for l in range(L):
                nc.vector.memset(m.par[:, l, 0:1], SLOPES[l])
                nc.vector.memset(m.par[:, l, 1:2], HAS_ELU[l])
            for n in range(G * NB):
                dve.wait_ge(adj_loaded[n % 6], 16 * (n // 6 + 1))
                nc.vector.tensor_scalar(m.mask[:, n // NB, n % NB, :], m.stage[:, n % 6, :], 0, EDGE, ALU.is_gt,
                                        ALU.mult, saturate=False).then_inc(masked, 1)
            dve.wait_ge(ident_ready, 1)
            nc.vector.tensor_copy(m.wall[:, 2, H_COL:], m.ident[0:D, 0:D])
            dve.wait_ge(w_loaded, 160)
            dve.wait_ge(wa_in_psum, 1)
            for c in range(2):
                last = nc.vector.tensor_copy(m.wall[:, :, c], m.ps[0:D, 0, 0:2 * L].rearrange(
                    "p (l c) -> p l c", c=2)[:, :, c])
            last.then_inc(wa_ready, 1)
            dve.wait_ge(wa_ready, 1)

        @block.tensor
        def _(pe):
            pe.wait_ge(w_loaded, 160)
            pe.wait_ge(ident_ready, 1)
            for l in range(L):
                wt = m.ident[0:D, 0:D] if l == 2 else m.wT[:, (0, 1, None, 2)[l], :]
                last = nc.tensor.matmul(m.ps[0:D, 0, 2 * l:2 * l + 2], wt, m.avec[:, l, :], start=True, stop=True,
                                        skip_group_check=True)
            last.then_inc(wa_in_psum, 1)


def gat_stack(nc, x, adjT, W0, W1, W3, WT0, WT1, WT3, a0, a1, a2, a3, out):
    with ExitStack() as ctx:
        m = place(nc, ctx)
        load(nc, m, x, adjT, (W0, W1, W3), (WT0, WT1, WT3), (a0, a1, a2, a3))
        general(nc, m, out)


def kernel(x, adj, L0_gnn_W, L0_gnn_a, L1_gnn_W, L1_gnn_a, L2_gnn_a, L3_gnn_W, L3_gnn_a):
    import numpy as _np
    import concourse.bacc as _bacc
    from concourse import mybir as _mybir
    from concourse.bass_utils import run_bass_kernel_spmd as _run

    nc = _bacc.Bacc("TRN2", target_bir_lowering=False, num_devices=1)
    given = {"x": x, "adjT": _np.asarray(adj).T, "W0": L0_gnn_W, "W1": L1_gnn_W, "W3": L3_gnn_W,
             "WT0": _np.asarray(L0_gnn_W).T, "WT1": _np.asarray(L1_gnn_W).T, "WT3": _np.asarray(L3_gnn_W).T,
             "a0": _np.asarray(L0_gnn_a).reshape(2, 64).T, "a1": _np.asarray(L1_gnn_a).reshape(2, 64).T,
             "a2": _np.asarray(L2_gnn_a).reshape(2, 64).T, "a3": _np.asarray(L3_gnn_a).reshape(2, 64).T}
    arrays, args = {}, []
    for name, value in given.items():
        a = _np.ascontiguousarray(value)
        arrays[f"in_{name}_dram"] = a
        args.append(nc.dram_tensor(f"in_{name}_dram", a.shape, _mybir.dt.from_np(a.dtype), kind="ExternalInput").ap())
    out = nc.dram_tensor("out_0_dram", (4096, 64), _mybir.dt.float32, kind="ExternalOutput").ap()
    gat_stack(nc, *args, out)
    r = _run(nc, [arrays], core_ids=[0])
    return r.results[0]["out_0_dram"]
```

```python
from contextlib import ExitStack

import concourse.bass as bass
from concourse import mybir
from concourse.alu_op_type import AluOpType as ALU

ACT = mybir.ActivationFunctionType
AX_X = mybir.AxisListType.X
F32 = mybir.dt.float32
F16 = mybir.dt.float16
FP8 = mybir.dt.float8e4
U8 = mybir.dt.uint8
I32 = mybir.dt.int32
RMAX = bass.bass_isa.ReduceOp.max

P = 128
N = 4096
D = 64
L = 4
NB = N // P
G = 8
GB = NB // G
GN = N // G
SLOPES = (0.2, 0.01, 0.01, 0.2)
HAS_ELU = (1.0, 1.0, 0.0, 1.0)
EPS = 1e-5
EDGE = 2.0
EDGE_BYTE = 64.0
S_COL, D_COL, H_COL = 0, 1, 2
PW = H_COL + D
EPI = 11

HSUM_AT = 13
SETUP_AT = 13
RECIP_AT, ELU_AT = 8, 10
CT = 2
NC = NB // CT
ERING = 4
SRING = 3
AHEAD = 12
VT = 4
NV = NB // VT
BANKS = 7
F = D + 1
UP = 1024.0
LOW = 4096.0
MAX_RANGE = 20.0
MAX_SQUARE = 3969.0


class Bag:
    pass


def place(nc, ctx):
    m = Bag()

    def sb(name, shape, dt):
        return ctx.enter_context(nc.sbuf_tensor(name, shape, dt))

    m.mask = sb("mask", [P, G, NB, GN], FP8)
    m.x = sb("x", [P, NB, D], F32)
    m.stage = sb("stage", [P, SRING, CT, GN], I32)
    m.proj = sb("proj", [P, NB, PW + 1], F32)
    m.xT = sb("xT", [D, GN], F32)
    m.vals = sb("vals", [P, NB * 4 * F], F16)
    m.srow = sb("srow", [P, G, GN], F32)
    m.edges = sb("edges", [P, ERING, CT, GN], FP8)
    m.nd = sb("nd", [P, GB, F], F32)
    m.sums = sb("sums", [P, 2, GB, 3 * F], F32)
    low = m.sums[:, 1, :, :].rearrange("p b n -> p (b n)")
    m.t0 = low[:, 0:GB * F].rearrange("p (b n) -> p b n", b=GB)
    m.t1 = low[:, GB * F:GB * (F + D)].rearrange("p (b n) -> p b n", b=GB)
    m.t2 = low[:, GB * (F + D):GB * (F + 2 * D)].rearrange("p (b n) -> p b n", b=GB)
    m.small = sb("small", [P, 8, GB], F32)
    m.halfneg = sb("halfneg", [P, GB], F32)
    m.ident = sb("ident", [P, P], F32)
    m.ones = sb("ones", [P, P], F32)
    m.wall = sb("wall", [D, L, PW], F32)
    m.avec = sb("avec", [D, L, 2], F32)
    m.par = sb("par", [P, L, 2], F32)
    m.wcur = sb("wcur", [D, PW], F32)
    m.wneg = sb("wneg", [D, P], F32)
    m.pcur = sb("pcur", [P, 2], F32)
    m.hsum = sb("hsum", [P, F], F32)
    m.hpart = sb("hpart", [P, GB, F], F32)
    m.cols = sb("cols", [P, 8, NB], F32)
    m.stats = sb("stats", [P, 32], F32)
    m.bad = sb("bad", [P, 1], I32)
    m.ps = ctx.enter_context(nc.psum_tensor("ps", [P, 8, 512], F32))
    return m


def apart(eng, turn):
    if not isinstance(turn, int):
        eng.nop(nofuse=True)



def general(nc, m, x, out):
    with ExitStack() as ctx:
        def sem(name):
            return ctx.enter_context(nc.semaphore("g_" + name))

        x_loaded = sem("x_loaded")
        par_ready = sem("par_ready")
        xT_in_psum = sem("xT_in_psum")
        xT_ready = sem("xT_ready")
        proj_in_psum = sem("proj_in_psum")
        proj_ready = sem("proj_ready")
        hsum_in_psum = sem("hsum_in_psum")
        hsum_ready = sem("hsum_ready")
        dneg_ready = sem("dneg_ready")
        dmin_ready = sem("dmin_ready")
        dve_step = sem("dve_step")
        acc_step = sem("acc_step")
        accT_in_psum = sem("accT_in_psum")
        chain = sem("chain")
        rows_in_psum = sem("rows_in_psum")
        rows_ready = sem("rows_ready")
        low_ready = sem("low_ready")
        score_ready = sem("score_ready")
        exp_ready = sem("exp_ready")
        prob_ready = sem("prob_ready")
        prob_used = sem("prob_used")
        epi = epilogue_semaphores(sem)
        out_done = sem("out_done")

        f = m.vals[:].bitcast(F32)

        def region(k, n=1):
            return f[:, k * GN:(k + n) * GN]

        acc = region(0)
        rows = region(1, 2).rearrange("p (r i) -> p r i", r=2)
        score = region(3, 2).rearrange("p (r i) -> p r i", r=2)
        prob = region(5, 2).rearrange("p (r i) -> p r i", r=2)
        diag = m.srow[:, 0:2, :]
        cols = m.srow[:, 2, :]
        dshift = cols[:, 0:NB]
        dslope = cols[:, NB:2 * NB]
        dneg = cols[:, 2 * NB:3 * NB]
        dnegmax = cols[:, 3 * NB:3 * NB + 1]
        dmin_neg = cols[:, 3 * NB + 1:3 * NB + 2]
        mu, q, top, r1, r2, q2 = (cols[:, 4 * NB + GB * k:4 * NB + GB * (k + 1)] for k in range(6))
        mask8 = m.mask[:].bitcast(U8)
        slope = m.pcur[:, 0:1]
        scol = m.proj[:, :, S_COL]
        dcol = m.proj[:, :, D_COL]
        block = ctx.enter_context(nc.Block())

        @block.tensor
        def _(pe):
            bad = pe.value_load(m.bad[0:1, 0:1], min_val=0, max_val=1)
            with pe.If(bad > 0):
                with pe.Fori(0, L) as l:
                    pe.wait_ge(par_ready, l + 1)
                    apart(pe, l)
                    pe.wait_ge(epi.x_ready, l * G + 1)
                    apart(pe, l)
                    for c in range(G):
                        if c >= 1:
                            pe.wait_ge(xT_ready, l * G + c)
                            apart(pe, l)
                        for b in range(GB):
                            last = nc.tensor.transpose(m.ps[0:D, 0, b * P:(b + 1) * P], m.x[:, c * GB + b, :], m.ident[:])
                        last.then_inc(xT_in_psum, 1)
                        pe.wait_ge(xT_ready, l * G + c + 1)
                        apart(pe, l)
                        if c >= 1:
                            pe.wait_ge(proj_ready, l * G + c)
                            apart(pe, l)
                        for b in range(GB):
                            last = nc.tensor.matmul(m.ps[:, 1, b * PW:(b + 1) * PW], m.xT[:, b * P:(b + 1) * P], m.wcur[:],
                                                    start=b == 0, stop=b == GB - 1, skip_group_check=True)
                        last.then_inc(proj_in_psum, 1)
                    pe.wait_ge(proj_ready, l * G + G)
                    apart(pe, l)
                    for b in range(NB):
                        last = nc.tensor.matmul(m.ps[:, 2, 0:D + 1], m.ones[:], m.proj[:, b, H_COL:],
                                                start=b == 0, stop=b == NB - 1)
                    last.then_inc(hsum_in_psum, 1)
                    with pe.Fori(0, G) as g:
                        k = l * G + g
                        pe.wait_ge(acc_step, k * NB + NB)
                        apart(pe, k)
                        for b in range(GB):
                            last = nc.tensor.transpose(m.ps[:, 3, b * P:(b + 1) * P], acc[:, b * P:(b + 1) * P], m.ident[:])
                        last.then_inc(accT_in_psum, 1)
                        pe.wait_ge(chain, k * 7 + 7)
                        apart(pe, k)
                        for r in range(2):
                            last = nc.tensor.matmul(m.ps[:, 4 + r, :], m.ones[:], diag[:, r, :], start=True, stop=True)
                        last.then_inc(rows_in_psum, 1)

                        def products(t, first):
                            for u in range(2):
                                pe.wait_ge(prob_ready, k * NB + t + u + 1)
                                apart(pe, k)
                                for b in range(GB):
                                    last = nc.tensor.matmul(
                                        m.ps[:, 6, b * (D + 1):(b + 1) * (D + 1)], prob[:, u, b * P:(b + 1) * P],
                                        m.proj[:, bass.ds(t + u, 1), H_COL:].rearrange("p a n -> p (a n)"),
                                        start=first and u == 0 and b == 0, stop=False, skip_group_check=True)
                                last.then_inc(prob_used, 1)

                        products(0, True)
                        with pe.Fori(1, NB // 2) as pair:
                            products(2 * pair, False)

        @block.scalar
        def _(act):
            bad = act.value_load(m.bad[0:1, 0:1], min_val=0, max_val=1)
            with act.If(bad > 0):
                with act.Fori(0, L) as l:
                    for c in range(G):
                        act.wait_ge(xT_in_psum, l * G + c + 1)
                        apart(act, l)
                        if c >= 1:
                            act.wait_ge(proj_in_psum, l * G + c)
                            apart(act, l)
                        nc.scalar.copy(m.xT[:], m.ps[0:D, 0, :]).then_inc(xT_ready, 1)
                        act.wait_ge(proj_in_psum, l * G + c + 1)
                        apart(act, l)
                        nc.scalar.copy(m.proj[:, c * GB:(c + 1) * GB, 0:PW],
                                       m.ps[:, 1, 0:GB * PW].rearrange("p (b n) -> p b n", b=GB)).then_inc(proj_ready, 1)
                    act.wait_ge(hsum_in_psum, l + 1)
                    apart(act, l)
                    nc.scalar.copy(m.hsum[:], m.ps[:, 2, 0:D + 1]).then_inc(hsum_ready, 1)
                    act.wait_ge(dve_step, l * 3 + 3)
                    apart(act, l)
                    with act.Fori(0, G) as g:
                        k = l * G + g
                        act.wait_ge(rows_in_psum, k + 1)
                        apart(act, k)
                        nc.scalar.copy(rows, m.ps[:, 4:6, :]).then_inc(rows_ready, 1)
                        act.wait_ge(rows_ready, k + 1)
                        apart(act, k)
                        with act.Fori(0, NB // 2) as pair:
                            t = 2 * pair
                            for u in range(2):
                                n = k * NB + t + u
                                nc.scalar.activation(score[:, u, :], rows[:, 1, :], ACT.Identity,
                                                     bias=dslope[:, bass.ds(t + u, 1)]).then_inc(low_ready, 1)
                            for u in range(2):
                                n = k * NB + t + u
                                act.wait_ge(score_ready, n + 1)
                                apart(act, n)
                                nc.scalar.activation(prob[:, u, :], score[:, u, :], ACT.Exp).then_inc(exp_ready, 1)
                            act.wait_ge(exp_ready, k * NB + t + 2)
                            apart(act, k)
                            act.wait_ge(prob_used, k * NB + t + 2)
                            apart(act, k)
                        act.wait_ge(epi.x_ready, k + 1)
                        apart(act, k)
                        nc.scalar.copy(m.nd[:], m.ps[:, 6, 0:GB * (D + 1)].rearrange("p (b n) -> p b n", b=GB)
                                       ).then_inc(epi.nd_ready, 1)
                        epilogue_act(nc, act, m, epi, k)

        @block.vector
        def _(dve):
            bad = dve.value_load(m.bad[0:1, 0:1], min_val=0, max_val=1)
            with dve.If(bad > 0):
                with dve.Fori(0, L) as l:
                    nc.vector.tensor_copy(m.wcur[:], m.wall[:, bass.ds(l, 1), :].rearrange("p a n -> p (a n)"))
                    nc.vector.tensor_copy(m.pcur[:], m.par[:, bass.ds(l, 1), :].rearrange("p a n -> p (a n)")
                                          ).then_inc(par_ready, 1)
                    dve.wait_ge(par_ready, l + 1)
                    apart(dve, l)
                    dve.wait_ge(proj_ready, l * G + G)
                    apart(dve, l)
                    nc.vector.tensor_scalar(dneg, dcol, -1.0, None, ALU.mult).then_inc(dve_step, 1)
                    nc.vector.tensor_scalar(dslope, dcol, slope, None, ALU.mult)
                    dve.wait_ge(dve_step, l * 3 + 1)
                    apart(dve, l)
                    nc.vector.tensor_reduce(dnegmax, dneg, op=ALU.max, axis=AX_X).then_inc(dve_step, 1)
                    dve.wait_ge(dmin_ready, l + 1)
                    apart(dve, l)
                    nc.vector.tensor_scalar(dshift, dcol, dmin_neg, 1.0, ALU.add, ALU.add).then_inc(dve_step, 1)
                    dve.wait_ge(dve_step, l * 3 + 3)
                    apart(dve, l)
                    with dve.Fori(0, G) as g:
                        k = l * G + g
                        nc.vector.memset(acc, 0.0).then_inc(chain, 1)
                        dve.wait_ge(chain, k * 7 + 1)
                        apart(dve, k)
                        with dve.Fori(0, NB) as t:
                            nc.vector.scalar_tensor_tensor(
                                acc, mask8[:, bass.ds(g, 1), bass.ds(t, 1), :].rearrange("p a b n -> p (a b n)"),
                                dshift[:, bass.ds(t, 1)], acc, ALU.mult, ALU.max).then_inc(acc_step, 1)
                            dve.wait_ge(acc_step, k * NB + t + 1)
                            apart(dve, k)
                        dve.wait_ge(accT_in_psum, k + 1)
                        apart(dve, k)
                        nc.vector.tensor_reduce(mu, m.ps[:, 3, :].rearrange("p (b n) -> p b n", b=GB),
                                                op=ALU.max, axis=AX_X).then_inc(chain, 1)
                        dve.wait_ge(chain, k * 7 + 2)
                        apart(dve, k)
                        nc.vector.tensor_scalar(q2, mu, 1.0 / EDGE_BYTE, dmin_neg, ALU.mult, ALU.subtract
                                                ).then_inc(chain, 1)
                        dve.wait_ge(chain, k * 7 + 3)
                        apart(dve, k)
                        nc.vector.scalar_tensor_tensor(q, q2, -1.0, scol[:, bass.ds(g * GB, GB)], ALU.add, ALU.add
                                                       ).then_inc(chain, 1)
                        dve.wait_ge(chain, k * 7 + 4)
                        apart(dve, k)
                        nc.vector.scalar_tensor_tensor(top, q, slope, q, ALU.mult, ALU.max).then_inc(chain, 1)
                        dve.wait_ge(chain, k * 7 + 5)
                        apart(dve, k)
                        nc.vector.tensor_tensor(r1, scol[:, bass.ds(g * GB, GB)], top, ALU.subtract)
                        nc.vector.scalar_tensor_tensor(r2, scol[:, bass.ds(g * GB, GB)], slope, top, ALU.mult,
                                                       ALU.subtract).then_inc(chain, 1)
                        dve.wait_ge(chain, k * 7 + 6)
                        apart(dve, k)
                        for r, col in enumerate((r1, r2)):
                            for b in range(GB):
                                last = nc.vector.tensor_scalar(diag[:, r, b * P:(b + 1) * P], m.ident[:], col[:, b:b + 1],
                                                               None, ALU.mult)
                        last.then_inc(chain, 1)
                        dve.wait_ge(rows_ready, k + 1)
                        apart(dve, k)
                        with dve.Fori(0, NB // 2) as pair:
                            t = 2 * pair
                            for u in range(2):
                                n = k * NB + t + u
                                dve.wait_ge(low_ready, n + 1)
                                apart(dve, n)
                                nc.vector.scalar_tensor_tensor(score[:, u, :], rows[:, 0, :], dcol[:, bass.ds(t + u, 1)],
                                                               score[:, u, :], ALU.add, ALU.max).then_inc(score_ready, 1)
                            for u in range(2):
                                n = k * NB + t + u
                                dve.wait_ge(exp_ready, n + 1)
                                apart(dve, n)
                                nc.vector.scalar_tensor_tensor(
                                    prob[:, u, :],
                                    mask8[:, bass.ds(g, 1), bass.ds(t + u, 1), :].rearrange("p a b n -> p (a b n)"),
                                    3.2e38 / EDGE_BYTE, prob[:, u, :], ALU.mult, ALU.min).then_inc(prob_ready, 1)
                        epilogue_recip(nc, dve, m, epi, k)
                        epilogue_elu(nc, dve, m, epi, k)

        @block.gpsimd
        def _(pool):
            bad = pool.value_load(m.bad[0:1, 0:1], min_val=0, max_val=1)
            with pool.If(bad > 0):
                pool.wait_ge(x_loaded, 16)
                nc.gpsimd.sem_inc(epi.x_ready, 1)
                with pool.Fori(0, L) as l:
                    pool.wait_ge(dve_step, l * 3 + 2)
                    apart(pool, l)
                    nc.gpsimd.partition_all_reduce(dmin_neg, dnegmax, P, RMAX).then_inc(dmin_ready, 1)
                    pool.wait_ge(hsum_ready, l + 1)
                    apart(pool, l)
                    with pool.Fori(0, G) as g:
                        k = l * G + g
                        epilogue_pool(nc, pool, m, epi, k, m.x[:, bass.ds(g * GB, GB), :])

        @block.sync
        def _(sp):
            bad = sp.value_load(m.bad[0:1, 0:1], min_val=0, max_val=1)
            with sp.If(bad > 0):
                sp.dma_start(m.x[:], x.rearrange("(b p) f -> p b f", p=P)).then_inc(x_loaded, 16)
                sp.wait_ge(epi.x_ready, L * G + 1)
                sp.dma_start(out.rearrange("(b p) f -> p b f", p=P), m.x[:]).then_inc(out_done, 16)
                sp.wait_ge(out_done, 16)



def epilogue_semaphores(sem):
    e = Bag()
    e.nd_ready = sem("nd_ready")
    e.pool_step = sem("pool_step")
    e.recip_ready = sem("recip_ready")
    e.exp_min = sem("exp_min")
    e.elu_step = sem("elu_step")
    e.sum_ready = sem("sum_ready")
    e.var_ready = sem("var_ready")
    e.x_ready = sem("x_ready")
    return e


def epilogue_pool(nc, pool, m, e, k, x):
    s = m.small
    zero, recip, total, negmean, sqsum, var, rstd = (s[:, n, :] for n in range(7))

    def wide(v):
        return v.unsqueeze(2).to_broadcast([P, GB, D])

    step = k * EPI
    pool.wait_ge(e.nd_ready, k + 1)
    apart(pool, k)
    nc.gpsimd.tensor_scalar(zero, m.nd[:, :, D], 0.0, None, ALU.is_equal).then_inc(e.pool_step, 1)
    pool.wait_ge(e.pool_step, step + 1)
    apart(pool, k)
    nc.gpsimd.tensor_tensor(m.t0, zero.unsqueeze(2).to_broadcast([P, GB, D + 1]),
                            m.hsum[:].unsqueeze(1).to_broadcast([P, GB, D + 1]), ALU.mult).then_inc(e.pool_step, 1)
    pool.wait_ge(e.pool_step, step + 2)
    apart(pool, k)
    nc.gpsimd.tensor_tensor(m.nd[:], m.nd[:], m.t0, ALU.add).then_inc(e.pool_step, 1)
    pool.wait_ge(e.recip_ready, k + 1)
    apart(pool, k)
    h = m.t0[:, :, 0:D]
    nc.gpsimd.tensor_tensor(h, m.nd[:, :, 0:D], wide(recip), ALU.mult).then_inc(e.pool_step, 1)
    pool.wait_ge(e.pool_step, step + 4)
    apart(pool, k)
    nc.gpsimd.tensor_scalar(m.t1, h, 0.0, None, ALU.min).then_inc(e.pool_step, 1)
    y = m.nd[:, :, 0:D]
    nc.gpsimd.tensor_tensor(y, x, h, ALU.add).then_inc(e.pool_step, 1)
    pool.wait_ge(e.sum_ready, k + 1)
    apart(pool, k)
    nc.gpsimd.tensor_scalar(negmean, total, -1.0 / D, 0.0, ALU.mult, ALU.add).then_inc(e.pool_step, 1)
    pool.wait_ge(e.pool_step, step + 7)
    apart(pool, k)
    nc.gpsimd.tensor_tensor(m.t1, y, wide(negmean), ALU.add).then_inc(e.pool_step, 1)
    pool.wait_ge(e.var_ready, k + 1)
    apart(pool, k)
    nc.gpsimd.tensor_scalar(var, sqsum, 1.0 / D, EPS, ALU.mult, ALU.add).then_inc(e.pool_step, 1)
    pool.wait_ge(e.pool_step, step + 9)
    apart(pool, k)
    nc.gpsimd.tensor_tensor(rstd, var, m.halfneg[:], ALU.pow).then_inc(e.pool_step, 1)
    pool.wait_ge(e.pool_step, step + 10)
    apart(pool, k)
    nc.gpsimd.tensor_tensor(x, m.t1, wide(rstd), ALU.mult).then_inc(e.pool_step, 1)
    pool.wait_ge(e.pool_step, step + 11)
    apart(pool, k)
    nc.gpsimd.sem_inc(e.x_ready, 1)


def epilogue_act(nc, act, m, e, k):
    s = m.small
    zero, recip, total, negmean, sqsum, var, rstd = (s[:, n, :] for n in range(7))
    y = m.nd[:, :, 0:D]
    act.wait_ge(e.pool_step, k * EPI + 5)
    apart(act, k)
    nc.scalar.activation(m.t2, m.t1, ACT.Exp).then_inc(e.exp_min, 1)
    act.wait_ge(e.elu_step, k * 2 + 2)
    apart(act, k)
    for b in range(GB):
        last = nc.scalar.activation(m.t2[:, b, :], y[:, b, :], ACT.Identity, accum_out=total[:, b:b + 1])
    last.then_inc(e.sum_ready, 1)
    act.wait_ge(e.pool_step, k * EPI + 7)
    apart(act, k)
    act.wait_ge(e.sum_ready, k + 1)
    apart(act, k)
    for b in range(GB):
        last = nc.scalar.activation(m.t2[:, b, :], y[:, b, :], ACT.Square, bias=negmean[:, b:b + 1],
                                    accum_out=sqsum[:, b:b + 1])
    last.then_inc(e.var_ready, 1)


def epilogue_recip(nc, dve, m, e, k):
    dve.wait_ge(e.pool_step, k * EPI + 3)
    apart(dve, k)
    nc.vector.reciprocal(m.small[:, 1, :], m.nd[:, :, D]).then_inc(e.recip_ready, 1)


def epilogue_elu(nc, dve, m, e, k):
    y = m.nd[:, :, 0:D]
    dve.wait_ge(e.exp_min, k + 1)
    apart(dve, k)
    dve.wait_ge(e.pool_step, k * EPI + 6)
    apart(dve, k)
    nc.vector.scalar_tensor_tensor(m.t1, m.t2, -1.0, m.t1, ALU.add, ALU.subtract).then_inc(e.elu_step, 1)
    dve.wait_ge(e.elu_step, k * 2 + 1)
    apart(dve, k)
    nc.vector.scalar_tensor_tensor(y, m.t1, m.pcur[:, 1:2], y, ALU.mult, ALU.add).then_inc(e.elu_step, 1)
    dve.wait_ge(e.elu_step, k * 2 + 2)
    apart(dve, k)



def fast(nc, m, x_in, adjT, ws, wTs, avecs, out):
    with ExitStack() as ctx:
        def sem(name):
            return ctx.enter_context(nc.semaphore("f_" + name))

        x_loaded = sem("x_loaded")
        w_loaded = sem("w_loaded")
        adj_loaded = [sem(f"adj_loaded{n}") for n in range(SRING)]
        zeroed = sem("zeroed")
        ident_ready = sem("ident_ready")
        const_ready = sem("const_ready")
        wa_in_psum = sem("wa_in_psum")
        wa_ready = sem("wa_ready")
        w_ready = sem("w_ready")
        par_ready = sem("par_ready")
        masked = sem("masked")
        xT_in_psum = sem("xT_in_psum")
        xT_ready = sem("xT_ready")
        proj_in_psum = sem("proj_in_psum")
        proj_ready = sem("proj_ready")
        square_ready = sem("square_ready")
        srow_in_psum = sem("srow_in_psum")
        srow_ready = sem("srow_ready")
        stat_step = sem("stat_step")
        statT_in_psum = sem("statT_in_psum")
        glob_in_psum = sem("glob_in_psum")
        v_ready = sem("v_ready")
        u_ready = sem("u_ready")
        ulow_ready = sem("ulow_ready")
        val_ready = sem("val_ready")
        high_ready = sem("high_ready")
        low_ready = sem("low_ready")
        hpart_step = sem("hpart_step")
        hsum_in_psum = sem("hsum_in_psum")
        hsum_ready = sem("hsum_ready")
        edges_ready = sem("edges_ready")
        edges_used = sem("edges_used")
        sums_in_psum = sem("sums_in_psum")
        sums_read = sem("sums_read")
        add_step = sem("add_step")
        epi = epilogue_semaphores(sem)
        row_step = sem("row_step")
        bad_ready = sem("bad_ready")
        out_done = sem("out_done")
        STAT = 6

        m.wT = m.sums[0:D, 0, 0, 0:3 * D].rearrange("p (n c) -> p n c", n=3)
        vals = m.vals[:].rearrange("p (t k n) -> p t k n", t=NB, k=4)
        flat = m.sums[:].rearrange("p a b n -> p (a b n)")
        val32 = flat[:, 0:4 * VT * F].rearrange("p (r t n) -> p r t n", r=2, t=VT)
        val32up = flat[:, 4 * VT * F:6 * VT * F].rearrange("p (t n) -> p t n", t=VT)
        dcur, dm, q, top, v, vs, u, us = (m.cols[:, n, :] for n in range(8))
        slope = m.pcur[:, 0:1]
        fsquare = m.stats[:, 0:G]
        three = m.stats[:, G:G + 3]
        dmin = m.stats[:, G + 3:G + 4]
        rowmax = m.stats[0:3, G + 4:G + 5]
        diag3 = m.stats[0:3, G + 5:G + 8]
        glob = m.stats[:, G + 8:G + 11]
        over = m.stats[:, G + 11:G + 13]
        bad = m.stats[:, G + 13:G + 14]
        block = ctx.enter_context(nc.Block())

        def layers(eng, layer):
            layer(0, True, False)
            with eng.Fori(1, L - 1) as l:
                layer(l, False, False)
            layer(L - 1, False, True)

        @block.sync
        def _(sp):
            adj_v = adjT.rearrange("(c t p) (g i) -> g c p t i", p=P, g=G, t=CT)
            sp.dma_start(m.x[:], x_in.rearrange("(b p) f -> p b f", p=P)).then_inc(x_loaded, 16)
            for n, l in enumerate((0, 1, 3)):
                sp.dma_start(m.wall[:, l, H_COL:], ws[n]).then_inc(w_loaded, 16)
                sp.dma_start(m.wT[:, n, :], wTs[n]).then_inc(w_loaded, 16)
            for l in range(L):
                sp.dma_start(m.avec[:, l, :], avecs[l]).then_inc(w_loaded, 16)
            for n in range(G * NC):
                if n >= SRING:
                    sp.wait_ge(masked, n - SRING + 1)
                    sp.wait_ge(adj_loaded[n % SRING], 16 * (n // SRING))
                sp.dma_start(m.stage[:, n % SRING, :, :], adj_v[n // NC, n % NC]).then_inc(adj_loaded[n % SRING], 16)
            out_v = out.rearrange("(g b p) f -> g p b f", p=P, g=G)
            for g in range(G):
                sp.wait_ge(epi.x_ready, (L - 1) * G + g + 1)
                sp.dma_start(out_v[g], m.x[:, g * GB:(g + 1) * GB, :]).then_inc(out_done, 16)
            sp.wait_ge(out_done, 16 * G)

        @block.tensor
        def _(pe):
            pe.wait_ge(w_loaded, 160)
            pe.wait_ge(ident_ready, 1)
            for l in range(L):
                wt = m.ident[0:D, 0:D] if l == 2 else m.wT[:, (0, 1, None, 2)[l], :]
                last = nc.tensor.matmul(m.ps[0:D, 6, 2 * l:2 * l + 2], wt, m.avec[:, l, :], start=True, stop=True,
                                        skip_group_check=True)
            last.then_inc(wa_in_psum, 1)

            def transposes(n, g, bank, free):
                if not isinstance(free, int) or free >= 1:
                    pe.wait_ge(srow_ready, free)
                    apart(pe, free)
                for b in range(GB):
                    last = nc.tensor.transpose(m.ps[0:D, bank, b * P:(b + 1) * P], m.x[:, g * GB + b, :], m.ident[:])
                last.then_inc(xT_in_psum, 1)

            def project(n, g, bank):
                pe.wait_ge(xT_ready, n + 1)
                apart(pe, n)
                for b in range(GB):
                    last = nc.tensor.matmul(m.ps[:, bank, b * PW:(b + 1) * PW], m.xT[:, b * P:(b + 1) * P], m.wcur[:],
                                            start=b == 0, stop=b == GB - 1, skip_group_check=True)
                last.then_inc(proj_in_psum, 1)

            def spread_s(n, bank):
                pe.wait_ge(proj_ready, n + 1)
                apart(pe, n)
                nc.tensor.matmul(m.ps[:, bank, :], m.wneg[:], m.xT[:], start=True, stop=True).then_inc(srow_in_psum, 1)

            pe.wait_ge(x_loaded, 16)
            pe.wait_ge(w_ready, 1)
            for g in range(G):
                transposes(g, g, 3 * (g % 2), g - 1)
                project(g, g, 3 * (g % 2) + 1)
                spread_s(g, 3 * (g % 2) + 2)

            def layer(l, first, last_layer):
                pe.wait_ge(stat_step, l * STAT + 2)
                apart(pe, l)
                nc.tensor.transpose(m.ps[0:3, 7, 0:P], three, m.ident[:]).then_inc(statT_in_psum, 1)
                pe.wait_ge(stat_step, l * STAT + 4)
                apart(pe, l)
                nc.tensor.matmul(m.ps[:, 7, P:P + 3], m.ones[0:3, :], diag3, start=True, stop=True
                                 ).then_inc(glob_in_psum, 1)
                for g in range(G):
                    for c in range(NC):
                        pe.wait_ge(edges_ready, (l * G + g) * NC + c + 1)
                        apart(pe, l)
                        for t in range(c * CT, (c + 1) * CT):
                            if g == 0 and t % VT == 0:
                                pe.wait_ge(low_ready, l * NV + t // VT + 1)
                                apart(pe, l)
                            for b in range(GB):
                                block_i = g * GB + b
                                bank = block_i % BANKS
                                if t == 0 and block_i >= BANKS:
                                    pe.wait_ge(sums_read, l * NB + block_i - BANKS + 1)
                                    apart(pe, l)
                                i = slice(b * P, (b + 1) * P)
                                sums = m.ps[:, bank, 0:6 * F].rearrange("p (h n) -> p h n", h=2)
                                nc.tensor.matmul(sums[:, :, 0:2 * F], m.edges[:, c % ERING, t % CT, i],
                                                 m.vals[:, t * 4 * F:(t + 1) * 4 * F].rearrange("p (h n) -> p h n", h=2),
                                                 start=t == 0, stop=t == NB - 1, skip_group_check=True)
                                last = nc.tensor.matmul(sums[:, :, 2 * F:], m.mask[:, g, t, i], vals[:, t, 1::2, :],
                                                        start=False, stop=t == NB - 1, skip_group_check=True)
                                if t == NB - 1:
                                    last.then_inc(sums_in_psum, 1)
                                    last = None
                        if c < NC - 1:
                            last.then_inc(edges_used, 1)
                        if g == 0 and c == HSUM_AT:
                            pe.wait_ge(hpart_step, l * G + G)
                            apart(pe, l)
                            for b in range(GB):
                                hs = nc.tensor.matmul(m.ps[:, 7, 256:256 + F], m.ones[:], m.hpart[:, b, :],
                                                      start=b == 0, stop=b == GB - 1)
                            hs.then_inc(hsum_in_psum, 1)
                        if g >= 1 and not last_layer:
                            n = (l + 1) * G + g - 1
                            if c == SETUP_AT:
                                pe.wait_ge(epi.x_ready, l * G + g)
                                apart(pe, l)
                                transposes(n, g - 1, 7, n)
                            if c == SETUP_AT + 1:
                                pe.wait_ge(w_ready, l + 2)
                                apart(pe, l)
                                project(n, g - 1, 7)
                            if c == SETUP_AT + 2:
                                spread_s(n, 7)
                if not last_layer:
                    pe.wait_ge(epi.x_ready, l * G + G)
                    apart(pe, l)
                    n = (l + 1) * G + G - 1
                    transposes(n, G - 1, 4, n)
                    project(n, G - 1, 5)
                    spread_s(n, 6)

            layers(pe, layer)

        @block.scalar
        def _(act):
            def copy_xT(n, bank):
                act.wait_ge(xT_in_psum, n + 1)
                apart(act, n)
                if not isinstance(n, int) or n >= 1:
                    act.wait_ge(srow_in_psum, n)
                    apart(act, n)
                nc.scalar.copy(m.xT[:], m.ps[0:D, bank, :]).then_inc(xT_ready, 1)

            def copy_proj(n, g, bank):
                act.wait_ge(proj_in_psum, n + 1)
                apart(act, n)
                nc.scalar.copy(m.proj[:, g * GB:(g + 1) * GB, 0:PW],
                               m.ps[:, bank, 0:GB * PW].rearrange("p (b n) -> p b n", b=GB)).then_inc(proj_ready, 1)
                act.wait_ge(proj_ready, n + 1)
                apart(act, n)
                if not isinstance(n, int) or n >= 1:
                    act.wait_ge(square_ready, n)
                    apart(act, n)
                nc.scalar.activation(m.t2, m.proj[:, g * GB:(g + 1) * GB, H_COL:PW], ACT.Square,
                                     accum_out=fsquare[:, g:g + 1]).then_inc(square_ready, 1)

            def copy_srow(n, g, bank):
                act.wait_ge(srow_in_psum, n + 1)
                apart(act, n)
                nc.scalar.copy(m.srow[:, g, :], m.ps[:, bank, :]).then_inc(srow_ready, 1)

            act.wait_ge(x_loaded, 16)
            for g in range(G):
                copy_xT(g, 3 * (g % 2))
                copy_proj(g, g, 3 * (g % 2) + 1)
                copy_srow(g, g, 3 * (g % 2) + 2)

            def layer(l, first, last_layer):
                act.wait_ge(stat_step, l * STAT + 6)
                apart(act, l)
                nc.scalar.activation(v, dm, ACT.Exp)
                nc.scalar.activation(vs, dm, ACT.Exp, scale=slope).then_inc(v_ready, 1)
                for k in range(NV):
                    n = l * NV + k
                    act.wait_ge(val_ready, n + 1)
                    apart(act, n)
                    nc.scalar.activation(vals[:, k * VT:(k + 1) * VT, 0:2, :].rearrange("p t k n -> p t (k n)"),
                                         val32[:, k % 2, :, :], ACT.Copy, scale=UP)
                    if k >= 1:
                        act.wait_ge(low_ready, n)
                        apart(act, n)
                    nc.scalar.activation(val32up, val32[:, k % 2, :, :], ACT.Copy, scale=UP * LOW
                                         ).then_inc(high_ready, 1)
                    if k == 3:
                        act.wait_ge(row_step, l * 4 + 3)
                        apart(act, l)
                        nc.scalar.activation(u, u, ACT.Exp)
                        nc.scalar.activation(us, us, ACT.Exp).then_inc(u_ready, 1)
                for g in range(G):
                    kk = l * G + g
                    if g == 0:
                        act.wait_ge(hsum_in_psum, l + 1)
                        apart(act, l)
                        nc.scalar.copy(m.hsum[:], m.ps[:, 7, 256:256 + F]).then_inc(hsum_ready, 1)
                        act.wait_ge(ulow_ready, l + 1)
                        apart(act, l)
                    if g >= 1 or not first:
                        act.wait_ge(epi.x_ready, kk)
                        apart(act, kk)
                    if g >= 1 and not last_layer:
                        act.wait_ge(square_ready, (l + 1) * G + g)
                        apart(act, l)
                    for b in range(GB):
                        block_i = g * GB + b
                        bank = block_i % BANKS
                        act.wait_ge(sums_in_psum, l * NB + block_i + 1)
                        apart(act, l)
                        psum = m.ps[:, bank, 0:6 * F].rearrange("p (h n) -> p h n", h=2)
                        for h, (uu, uus) in enumerate(((u, us), (q, top))):
                            nc.scalar.activation(m.sums[:, h, b, 0:F], psum[:, h, 0:F], ACT.Copy,
                                                 scale=uu[:, block_i:block_i + 1])
                            last = nc.scalar.activation(m.sums[:, h, b, F:], psum[:, h, F:], ACT.Copy,
                                                        scale=uus[:, block_i:block_i + 1])
                        last.then_inc(sums_read, 1)
                    epilogue_act(nc, act, m, epi, kk)
                    if not last_layer:
                        n = (l + 1) * G + g
                        banks = (7, 7, 7) if g < G - 1 else (4, 5, 6)
                        copy_xT(n, banks[0])
                        copy_proj(n, g, banks[1])
                        copy_srow(n, g, banks[2])

            layers(act, layer)

        @block.vector
        def _(dve):
            nc.vector.memset(m.ones[:], 1.0)
            nc.vector.memset(m.halfneg[:], -0.5)
            nc.vector.memset(m.proj[:, :, PW], 1.0)
            nc.vector.memset(bad, 0.0)
            for l in range(L):
                nc.vector.memset(m.par[:, l, 0:1], SLOPES[l])
                last = nc.vector.memset(m.par[:, l, 1:2], HAS_ELU[l])
            last.then_inc(const_ready, 1)
            dve.wait_ge(const_ready, 1)

            def make_mask(n):
                if n < G * NC:
                    dve.wait_ge(adj_loaded[n % SRING], 16 * (n // SRING + 1))
                    apart(dve, n)
                    c = n % NC
                    nc.vector.tensor_scalar(m.mask[:, n // NC, c * CT:(c + 1) * CT, :], m.stage[:, n % SRING, :, :],
                                            0, EDGE, ALU.is_gt, ALU.mult, saturate=False).then_inc(masked, 1)

            def weights(l):
                nc.vector.tensor_copy(m.wcur[:], m.wall[:, bass.ds(l, 1), :].rearrange("p a n -> p (a n)"))
                nc.vector.tensor_scalar(m.wneg[:], m.ones[0:D, :],
                                        m.wall[:, bass.ds(l, 1), S_COL:S_COL + 1].rearrange("p a n -> p (a n)"), -1.0,
                                        ALU.mult, ALU.mult).then_inc(w_ready, 1)

            dve.wait_ge(ident_ready, 1)
            nc.vector.tensor_copy(m.wall[:, 2, H_COL:], m.ident[0:D, 0:D])
            dve.wait_ge(w_loaded, 160)
            dve.wait_ge(wa_in_psum, 1)
            for c in range(2):
                last = nc.vector.tensor_copy(m.wall[:, :, c], m.ps[0:D, 6, 0:2 * L].rearrange(
                    "p (l c) -> p l c", c=2)[:, :, c])
            last.then_inc(wa_ready, 1)
            dve.wait_ge(wa_ready, 1)
            weights(0)
            for n in range(AHEAD):
                make_mask(n)

            def layer(l, first, last_layer):
                base = l * STAT
                dve.wait_ge(square_ready, l * G + G)
                apart(dve, l)
                nc.vector.tensor_copy(dcur, m.proj[:, :, D_COL])
                nc.vector.tensor_reduce(three[:, 0:1], m.proj[:, :, D_COL], op=ALU.max, axis=AX_X)
                nc.vector.tensor_reduce(dmin, m.proj[:, :, D_COL], op=ALU.min, axis=AX_X).then_inc(stat_step, 1)
                dve.wait_ge(stat_step, base + 1)
                apart(dve, l)
                nc.vector.tensor_reduce(three[:, 2:3], fsquare, op=ALU.max, axis=AX_X)
                nc.vector.tensor_scalar(three[:, 1:2], dmin, -1.0, None, ALU.mult).then_inc(stat_step, 1)
                nc.vector.tensor_copy(m.pcur[:], m.par[:, bass.ds(l, 1), :].rearrange("p a n -> p (a n)")
                                      ).then_inc(par_ready, 1)
                dve.wait_ge(statT_in_psum, l + 1)
                apart(dve, l)
                nc.vector.tensor_reduce(rowmax, m.ps[0:3, 7, 0:P], op=ALU.max, axis=AX_X).then_inc(stat_step, 1)
                dve.wait_ge(stat_step, base + 3)
                apart(dve, l)
                nc.vector.tensor_scalar(diag3, m.ident[0:3, 0:3], rowmax, None, ALU.mult).then_inc(stat_step, 1)
                dve.wait_ge(glob_in_psum, l + 1)
                apart(dve, l)
                nc.vector.tensor_copy(glob, m.ps[:, 7, P:P + 3]).then_inc(stat_step, 1)
                dve.wait_ge(stat_step, base + 5)
                apart(dve, l)
                nc.vector.tensor_scalar(dm, dcur, glob[:, 0:1], None, ALU.subtract).then_inc(stat_step, 1)

                def edges(g, c):
                    if first:
                        make_mask(g * NC + c + AHEAD)
                    n = (l * G + g) * NC + c
                    used_wait(g * NC + c - ERING)
                    if c == 0:
                        dve.wait_ge(srow_ready, l * G + g + 1)
                        apart(dve, l)
                    for t in range(c * CT, (c + 1) * CT):
                        last = nc.vector.scalar_tensor_tensor(
                            m.edges[:, c % ERING, t % CT, :], m.srow[:, g, :], dcur[:, t:t + 1], m.mask[:, g, t, :],
                            ALU.is_lt, ALU.mult, saturate=False)
                    last.then_inc(edges_ready, 1)

                def used_wait(back):
                    if first and back < 0:
                        return
                    g, c = divmod(back, NC)
                    if c == NC - 1:
                        dve.wait_ge(sums_in_psum, l * NB + (g + 1) * GB)
                        apart(dve, l)
                    else:
                        dve.wait_ge(edges_used, (l * G + g) * (NC - 1) + c + 1)
                        apart(dve, l)

                def low_part(k):
                    n = l * NV + k
                    dve.wait_ge(high_ready, n + 1)
                    apart(dve, n)
                    nc.vector.scalar_tensor_tensor(
                        vals[:, k * VT:(k + 1) * VT, 2:4, :].rearrange("p t k n -> p t (k n)"),
                        vals[:, k * VT:(k + 1) * VT, 0:2, :].rearrange("p t k n -> p t (k n)"),
                        -LOW, val32up, ALU.mult, ALU.add).then_inc(low_ready, 1)

                def row_factors():
                    nc.vector.tensor_scalar(q, m.proj[:, :, S_COL], glob[:, 0:1], None, ALU.add).then_inc(row_step, 1)
                    dve.wait_ge(row_step, l * 4 + 1)
                    apart(dve, l)
                    nc.vector.scalar_tensor_tensor(top, q, slope, q, ALU.mult, ALU.max).then_inc(row_step, 1)
                    dve.wait_ge(row_step, l * 4 + 2)
                    apart(dve, l)
                    nc.vector.scalar_tensor_tensor(us, q, slope, top, ALU.mult, ALU.subtract)
                    nc.vector.tensor_tensor(u, q, top, ALU.subtract).then_inc(row_step, 1)
                    nc.vector.tensor_scalar(over[:, 0:1], glob[:, 0:1], glob[:, 1:2], MAX_RANGE, ALU.add, ALU.is_gt)
                    nc.vector.tensor_scalar(over[:, 1:2], glob[:, 2:3], MAX_SQUARE, None, ALU.is_gt
                                            ).then_inc(row_step, 1)
                    dve.wait_ge(row_step, l * 4 + 4)
                    apart(dve, l)
                    nc.vector.scalar_tensor_tensor(bad, over[:, 0:1], bad, over[:, 1:2], ALU.max, ALU.max)

                for g in range(G):
                    for c in range(NC):
                        edges(g, c)
                        if g == 0:
                            if c % 2 == 1:
                                low_part(c // 2)
                            if c == 3:
                                row_factors()
                            if c == 8:
                                dve.wait_ge(u_ready, l + 1)
                                apart(dve, l)
                                nc.vector.tensor_scalar(q, u, 1.0 / LOW, None, ALU.mult)
                                nc.vector.tensor_scalar(top, us, 1.0 / LOW, None, ALU.mult).then_inc(ulow_ready, 1)
                            if c == 12 and not last_layer:
                                dve.wait_ge(srow_ready, l * G + G)
                                apart(dve, l)
                                weights(l + 1)
                        if g >= 1:
                            if c == RECIP_AT:
                                epilogue_recip(nc, dve, m, epi, l * G + g - 1)
                            if c == ELU_AT:
                                epilogue_elu(nc, dve, m, epi, l * G + g - 1)
                epilogue_recip(nc, dve, m, epi, l * G + G - 1)
                epilogue_elu(nc, dve, m, epi, l * G + G - 1)

            layers(dve, layer)
            dve.wait_ge(row_step, L * 4)
            nc.vector.tensor_copy(m.bad[:], bad).then_inc(bad_ready, 1)
            dve.wait_ge(bad_ready, 1)

        @block.gpsimd
        def _(pool):
            nc.gpsimd.memset(m.ident[:], 0.0).then_inc(zeroed, 1)
            pool.wait_ge(zeroed, 1)
            nc.gpsimd.affine_select(out=m.ident[:], in_=m.ident[:], compare_op=ALU.not_equal, fill=1.0, base=0,
                                    pattern=[[-1, P]], channel_multiplier=1).then_inc(ident_ready, 1)
            pool.wait_ge(const_ready, 1)

            def layer(l, first, last_layer):
                pool.wait_ge(v_ready, l + 1)
                apart(pool, l)
                for k in range(NV):
                    n = l * NV + k
                    t = slice(k * VT, (k + 1) * VT)
                    if k >= 2:
                        pool.wait_ge(high_ready, n - 1)
                        apart(pool, n)
                    for c, col in enumerate((v, vs)):
                        last = nc.gpsimd.tensor_tensor(val32[:, k % 2, :, c * F:(c + 1) * F], m.proj[:, t, H_COL:],
                                                       col[:, t].unsqueeze(2).to_broadcast([P, VT, F]), ALU.mult)
                    last.then_inc(val_ready, 1)
                for g in range(1, G):
                    a = m.proj[:, 0:GB, H_COL:] if g == 1 else m.hpart[:]
                    if g >= 2:
                        pool.wait_ge(hpart_step, l * G + g - 1)
                        apart(pool, l)
                    nc.gpsimd.tensor_tensor(m.hpart[:], a, m.proj[:, g * GB:(g + 1) * GB, H_COL:], ALU.add
                                            ).then_inc(hpart_step, 1 if g < G - 1 else 2)
                pool.wait_ge(hsum_ready, l + 1)
                apart(pool, l)
                for g in range(G):
                    kk = l * G + g
                    pool.wait_ge(sums_read, l * NB + (g + 1) * GB)
                    apart(pool, l)
                    high, low = m.sums[:, 0, :, :], m.sums[:, 1, :, :]
                    nc.gpsimd.tensor_tensor(high, high, low, ALU.add).then_inc(add_step, 1)
                    pool.wait_ge(add_step, kk * 3 + 1)
                    apart(pool, kk)
                    nc.gpsimd.tensor_tensor(m.nd[:], high[:, :, 2 * F:], high[:, :, F:2 * F], ALU.subtract
                                            ).then_inc(add_step, 1)
                    pool.wait_ge(add_step, kk * 3 + 2)
                    apart(pool, kk)
                    nc.gpsimd.tensor_tensor(m.nd[:], m.nd[:], high[:, :, 0:F], ALU.add).then_inc(add_step, 1)
                    pool.wait_ge(add_step, kk * 3 + 3)
                    apart(pool, kk)
                    nc.gpsimd.sem_inc(epi.nd_ready, 1)
                    epilogue_pool(nc, pool, m, epi, kk, m.x[:, g * GB:(g + 1) * GB, :])

            layers(pool, layer)


def gat_stack(nc, x, adjT, W0, W1, W3, WT0, WT1, WT3, a0, a1, a2, a3, out):
    with ExitStack() as ctx:
        m = place(nc, ctx)
        fast(nc, m, x, adjT, (W0, W1, W3), (WT0, WT1, WT3), (a0, a1, a2, a3), out)
        general(nc, m, x, out)


def kernel(x, adj, L0_gnn_W, L0_gnn_a, L1_gnn_W, L1_gnn_a, L2_gnn_a, L3_gnn_W, L3_gnn_a):
    import numpy as _np
    import concourse.bacc as _bacc
    from concourse import mybir as _mybir
    from concourse.bass_utils import run_bass_kernel_spmd as _run

    nc = _bacc.Bacc("TRN2", target_bir_lowering=False, num_devices=1)
    given = {"x": x, "adjT": _np.asarray(adj).T, "W0": L0_gnn_W, "W1": L1_gnn_W, "W3": L3_gnn_W,
             "WT0": _np.asarray(L0_gnn_W).T, "WT1": _np.asarray(L1_gnn_W).T, "WT3": _np.asarray(L3_gnn_W).T,
             "a0": _np.asarray(L0_gnn_a).reshape(2, 64).T, "a1": _np.asarray(L1_gnn_a).reshape(2, 64).T,
             "a2": _np.asarray(L2_gnn_a).reshape(2, 64).T, "a3": _np.asarray(L3_gnn_a).reshape(2, 64).T}
    arrays, args = {}, []
    for name, value in given.items():
        a = _np.ascontiguousarray(value)
        arrays[f"in_{name}_dram"] = a
        args.append(nc.dram_tensor(f"in_{name}_dram", a.shape, _mybir.dt.from_np(a.dtype), kind="ExternalInput").ap())
    out = nc.dram_tensor("out_0_dram", (4096, 64), _mybir.dt.float32, kind="ExternalOutput").ap()
    gat_stack(nc, *args, out)
    r = _run(nc, [arrays], core_ids=[0])
    return r.results[0]["out_0_dram"]
```

```python
from contextlib import ExitStack

import concourse.bass as bass
from concourse import mybir
from concourse.alu_op_type import AluOpType as ALU

ACT = mybir.ActivationFunctionType
AX_X = mybir.AxisListType.X
F32 = mybir.dt.float32
F16 = mybir.dt.float16
FP8 = mybir.dt.float8e4
U8 = mybir.dt.uint8
U32 = mybir.dt.uint32
I32 = mybir.dt.int32
RMAX = bass.bass_isa.ReduceOp.max

P = 128
N = 4096
D = 64
L = 4
NB = N // P
G = 8
GB = NB // G
GN = N // G
SLOPES = (0.2, 0.01, 0.01, 0.2)
HAS_ELU = (1.0, 1.0, 0.0, 1.0)
EPS = 1e-5
EDGE = 2.0
EDGE_BYTE = 64.0
EDGE_WORD = 0x40404040
S_COL, D_COL, H_COL = 0, 1, 2
PW = H_COL + D
EPI = 12

CT = 2
NC = NB // CT
ERING = 4
TRING = 8
SRING = 3
AHEAD = 8
VT = 4
NV = NB // VT
EARLY = 24
XPARTS = 4
BANKS = 7
F = D + 1
UP = 128.0
LOW = 4096.0
MAX_RANGE = 18.0
MAX_ABOVE = 2.0
MAX_SQUARE = 4761.0
K = 2.0 ** 40
ACT_TILES_FIRST = (2, 2, 1, 2)
ACT_TILES = (1, 2, 1, 2)
SETUP_AT, COPY_AT = (2, 3, 4, 5, 7), (8, 10)
SPREAD_AT, SROW_AT = (9, 10, 11, 12), 15
EVACUATE_AT = 3
HSUM_AT, HCOPY_AT = 1, 4
RECIP_AT, EXP_AT, ELU_AT, VARIANCE_AT = 10, 12, 12, 14
SETUP_SOON, EVACUATE_SOON = (1, 2, 3, 4, 6), 3
RECIP_SOON, EXP_SOON, ELU_SOON, VARIANCE_SOON = 7, 11, 11, 12
DMAX_AT, V_AT = 8, 11
SPLIT_AT, LOWS_AT = (12, 13, 14, 15), (14, 15)
SHIFT_AT, LOW6_AT = 9, 12
LATE_AT = 13


class Bag:
    pass


def place(nc, ctx):
    m = Bag()

    def sb(name, shape, dt):
        return ctx.enter_context(nc.sbuf_tensor(name, shape, dt))

    m.mask = sb("mask", [P, G, NB, GN], FP8)
    m.x = sb("x", [P, NB, D], F32)
    m.stage = sb("stage", [P, SRING, CT, GN], I32)
    m.proj = sb("proj", [P, NB, PW + 1], F32)
    m.shared = sb("shared", [P, 2 * VT * F], F32)
    m.xT = m.shared[0:D, 0:GN]
    m.t2 = m.shared[:, 0:GB * D].rearrange("p (b n) -> p b n", b=GB)
    m.squared = m.t2
    m.vals = sb("vals", [P, NB * 4 * F], F16)
    m.srow = sb("srow", [P, 2, GN], F32)
    m.steps = sb("steps", [P, TRING, CT, GN], FP8)
    m.edges = sb("edges", [P, ERING, 2, CT, GN], FP8)
    m.nd = sb("nd", [P, GB, F], F32)
    m.sums = sb("sums", [P, 4, GB, F], F32)
    low = m.sums[:, 2:4, :, :].rearrange("p a b n -> p (a b n)")
    m.t0 = low[:, 0:GB * F].rearrange("p (b n) -> p b n", b=GB)
    m.t1 = low[:, GB * F:GB * (F + D)].rearrange("p (b n) -> p b n", b=GB)
    m.small = sb("small", [P, 8, GB], F32)
    m.halfneg = sb("halfneg", [P, GB], F32)
    m.ident = sb("ident", [P, P], F32)
    m.ones = sb("ones", [P, P], F32)
    m.wall = sb("wall", [D, L, PW], F32)
    m.par = sb("par", [P, L, 2], F32)
    m.wcur = sb("wcur", [D, PW], F32)
    m.pcur = sb("pcur", [P, 2], F32)
    m.hsum = sb("hsum", [P, F], F32)
    m.cols = sb("cols", [P, 9, NB], F32)
    m.stats = sb("stats", [P, 32], F32)
    m.bad = sb("bad", [P, 1], I32)
    m.ps = ctx.enter_context(nc.psum_tensor("ps", [P, 8, 512], F32))
    return m


def apart(eng, turn):
    if not isinstance(turn, int):
        eng.nop(nofuse=True)



def general(nc, m, x, out):
    with ExitStack() as ctx:
        def sem(name):
            return ctx.enter_context(nc.semaphore("g_" + name))

        x_loaded = sem("x_loaded")
        par_ready = sem("par_ready")
        xT_in_psum = sem("xT_in_psum")
        xT_ready = sem("xT_ready")
        proj_in_psum = sem("proj_in_psum")
        proj_ready = sem("proj_ready")
        hsum_in_psum = sem("hsum_in_psum")
        hsum_ready = sem("hsum_ready")
        dneg_ready = sem("dneg_ready")
        dmin_ready = sem("dmin_ready")
        dve_step = sem("dve_step")
        acc_step = sem("acc_step")
        accT_in_psum = sem("accT_in_psum")
        chain = sem("chain")
        rows_in_psum = sem("rows_in_psum")
        rows_ready = sem("rows_ready")
        low_ready = sem("low_ready")
        score_ready = sem("score_ready")
        exp_ready = sem("exp_ready")
        prob_ready = sem("prob_ready")
        prob_used = sem("prob_used")
        epi = epilogue_semaphores(sem)
        out_done = sem("out_done")

        f = m.vals[:].bitcast(F32)

        def region(k, n=1):
            return f[:, k * GN:(k + n) * GN]

        acc = region(0)
        rows = region(1, 2).rearrange("p (r i) -> p r i", r=2)
        score = region(3, 2).rearrange("p (r i) -> p r i", r=2)
        prob = region(5, 2).rearrange("p (r i) -> p r i", r=2)
        stage = m.stage[:].bitcast(F32).rearrange("p a t n -> p (a t) n")
        diag = stage[:, 0:2, :]
        cols = stage[:, 2, :]
        dshift = cols[:, 0:NB]
        dslope = cols[:, NB:2 * NB]
        dneg = cols[:, 2 * NB:3 * NB]
        dnegmax = cols[:, 3 * NB:3 * NB + 1]
        dmin_neg = cols[:, 3 * NB + 1:3 * NB + 2]
        mu, q, top, r1, r2, q2 = (cols[:, 4 * NB + GB * k:4 * NB + GB * (k + 1)] for k in range(6))
        mask8 = m.mask[:].bitcast(U8)
        slope = m.pcur[:, 0:1]
        scol = m.proj[:, :, S_COL]
        dcol = m.proj[:, :, D_COL]
        block = ctx.enter_context(nc.Block())

        @block.tensor
        def _(pe):
            bad = pe.value_load(m.bad[0:1, 0:1], min_val=0, max_val=1)
            with pe.If(bad > 0):
                with pe.Fori(0, L) as l:
                    pe.wait_ge(par_ready, l + 1)
                    apart(pe, l)
                    pe.wait_ge(epi.x_ready, l * G + 1)
                    apart(pe, l)
                    for c in range(G):
                        if c >= 1:
                            pe.wait_ge(xT_ready, l * G + c)
                            apart(pe, l)
                        for b in range(GB):
                            last = nc.tensor.transpose(m.ps[0:D, 0, b * P:(b + 1) * P], m.x[:, c * GB + b, :], m.ident[:])
                        last.then_inc(xT_in_psum, 1)
                        pe.wait_ge(xT_ready, l * G + c + 1)
                        apart(pe, l)
                        if c >= 1:
                            pe.wait_ge(proj_ready, l * G + c)
                            apart(pe, l)
                        for b in range(GB):
                            last = nc.tensor.matmul(m.ps[:, 1, b * PW:(b + 1) * PW], m.xT[:, b * P:(b + 1) * P], m.wcur[:],
                                                    start=b == 0, stop=b == GB - 1, skip_group_check=True)
                        last.then_inc(proj_in_psum, 1)
                    pe.wait_ge(proj_ready, l * G + G)
                    apart(pe, l)
                    for b in range(NB):
                        last = nc.tensor.matmul(m.ps[:, 2, 0:D + 1], m.ones[:], m.proj[:, b, H_COL:],
                                                start=b == 0, stop=b == NB - 1)
                    last.then_inc(hsum_in_psum, 1)
                    with pe.Fori(0, G) as g:
                        k = l * G + g
                        pe.wait_ge(acc_step, k * NB + NB)
                        apart(pe, k)
                        for b in range(GB):
                            last = nc.tensor.transpose(m.ps[:, 3, b * P:(b + 1) * P], acc[:, b * P:(b + 1) * P], m.ident[:])
                        last.then_inc(accT_in_psum, 1)
                        pe.wait_ge(chain, k * 7 + 7)
                        apart(pe, k)
                        for r in range(2):
                            last = nc.tensor.matmul(m.ps[:, 4 + r, :], m.ones[:], diag[:, r, :], start=True, stop=True)
                        last.then_inc(rows_in_psum, 1)

                        def products(t, first):
                            for u in range(2):
                                pe.wait_ge(prob_ready, k * NB + t + u + 1)
                                apart(pe, k)
                                for b in range(GB):
                                    last = nc.tensor.matmul(
                                        m.ps[:, 6, b * (D + 1):(b + 1) * (D + 1)], prob[:, u, b * P:(b + 1) * P],
                                        m.proj[:, bass.ds(t + u, 1), H_COL:].rearrange("p a n -> p (a n)"),
                                        start=first and u == 0 and b == 0, stop=False, skip_group_check=True)
                                last.then_inc(prob_used, 1)

                        products(0, True)
                        with pe.Fori(1, NB // 2) as pair:
                            products(2 * pair, False)

        @block.scalar
        def _(act):
            bad = act.value_load(m.bad[0:1, 0:1], min_val=0, max_val=1)
            with act.If(bad > 0):
                with act.Fori(0, L) as l:
                    for c in range(G):
                        act.wait_ge(xT_in_psum, l * G + c + 1)
                        apart(act, l)
                        if c >= 1:
                            act.wait_ge(proj_in_psum, l * G + c)
                            apart(act, l)
                        nc.scalar.copy(m.xT, m.ps[0:D, 0, :]).then_inc(xT_ready, 1)
                        act.wait_ge(proj_in_psum, l * G + c + 1)
                        apart(act, l)
                        nc.scalar.copy(m.proj[:, c * GB:(c + 1) * GB, 0:PW],
                                       m.ps[:, 1, 0:GB * PW].rearrange("p (b n) -> p b n", b=GB)).then_inc(proj_ready, 1)
                    act.wait_ge(hsum_in_psum, l + 1)
                    apart(act, l)
                    nc.scalar.copy(m.hsum[:], m.ps[:, 2, 0:D + 1]).then_inc(hsum_ready, 1)
                    act.wait_ge(dve_step, l * 3 + 3)
                    apart(act, l)
                    with act.Fori(0, G) as g:
                        k = l * G + g
                        act.wait_ge(rows_in_psum, k + 1)
                        apart(act, k)
                        nc.scalar.copy(rows, m.ps[:, 4:6, :]).then_inc(rows_ready, 1)
                        act.wait_ge(rows_ready, k + 1)
                        apart(act, k)
                        with act.Fori(0, NB // 2) as pair:
                            t = 2 * pair
                            for u in range(2):
                                n = k * NB + t + u
                                nc.scalar.activation(score[:, u, :], rows[:, 1, :], ACT.Identity,
                                                     bias=dslope[:, bass.ds(t + u, 1)]).then_inc(low_ready, 1)
                            for u in range(2):
                                n = k * NB + t + u
                                act.wait_ge(score_ready, n + 1)
                                apart(act, n)
                                nc.scalar.activation(prob[:, u, :], score[:, u, :], ACT.Exp).then_inc(exp_ready, 1)
                            act.wait_ge(exp_ready, k * NB + t + 2)
                            apart(act, k)
                            act.wait_ge(prob_used, k * NB + t + 2)
                            apart(act, k)
                        act.wait_ge(epi.x_ready, k + 1)
                        apart(act, k)
                        nc.scalar.copy(m.nd[:], m.ps[:, 6, 0:GB * (D + 1)].rearrange("p (b n) -> p b n", b=GB)
                                       ).then_inc(epi.nd_ready, 1)
                        epilogue_exp(nc, act, m, epi, k)

        @block.vector
        def _(dve):
            bad = dve.value_load(m.bad[0:1, 0:1], min_val=0, max_val=1)
            with dve.If(bad > 0):
                with dve.Fori(0, L) as l:
                    nc.vector.tensor_copy(m.wcur[:], m.wall[:, bass.ds(l, 1), :].rearrange("p a n -> p (a n)"))
                    nc.vector.tensor_copy(m.pcur[:], m.par[:, bass.ds(l, 1), :].rearrange("p a n -> p (a n)")
                                          ).then_inc(par_ready, 1)
                    dve.wait_ge(par_ready, l + 1)
                    apart(dve, l)
                    dve.wait_ge(proj_ready, l * G + G)
                    apart(dve, l)
                    nc.vector.tensor_scalar(dneg, dcol, -1.0, None, ALU.mult).then_inc(dve_step, 1)
                    nc.vector.tensor_scalar(dslope, dcol, slope, None, ALU.mult)
                    dve.wait_ge(dve_step, l * 3 + 1)
                    apart(dve, l)
                    nc.vector.tensor_reduce(dnegmax, dneg, op=ALU.max, axis=AX_X).then_inc(dve_step, 1)
                    dve.wait_ge(dmin_ready, l + 1)
                    apart(dve, l)
                    nc.vector.tensor_scalar(dshift, dcol, dmin_neg, 1.0, ALU.add, ALU.add).then_inc(dve_step, 1)
                    dve.wait_ge(dve_step, l * 3 + 3)
                    apart(dve, l)
                    with dve.Fori(0, G) as g:
                        k = l * G + g
                        nc.vector.memset(acc, 0.0).then_inc(chain, 1)
                        dve.wait_ge(chain, k * 7 + 1)
                        apart(dve, k)
                        with dve.Fori(0, NB) as t:
                            nc.vector.scalar_tensor_tensor(
                                acc, mask8[:, bass.ds(g, 1), bass.ds(t, 1), :].rearrange("p a b n -> p (a b n)"),
                                dshift[:, bass.ds(t, 1)], acc, ALU.mult, ALU.max).then_inc(acc_step, 1)
                            dve.wait_ge(acc_step, k * NB + t + 1)
                            apart(dve, k)
                        dve.wait_ge(accT_in_psum, k + 1)
                        apart(dve, k)
                        nc.vector.tensor_reduce(mu, m.ps[:, 3, :].rearrange("p (b n) -> p b n", b=GB),
                                                op=ALU.max, axis=AX_X).then_inc(chain, 1)
                        dve.wait_ge(chain, k * 7 + 2)
                        apart(dve, k)
                        nc.vector.tensor_scalar(q2, mu, 1.0 / EDGE_BYTE, dmin_neg, ALU.mult, ALU.subtract
                                                ).then_inc(chain, 1)
                        dve.wait_ge(chain, k * 7 + 3)
                        apart(dve, k)
                        nc.vector.scalar_tensor_tensor(q, q2, -1.0, scol[:, bass.ds(g * GB, GB)], ALU.add, ALU.add
                                                       ).then_inc(chain, 1)
                        dve.wait_ge(chain, k * 7 + 4)
                        apart(dve, k)
                        nc.vector.scalar_tensor_tensor(top, q, slope, q, ALU.mult, ALU.max).then_inc(chain, 1)
                        dve.wait_ge(chain, k * 7 + 5)
                        apart(dve, k)
                        nc.vector.tensor_tensor(r1, scol[:, bass.ds(g * GB, GB)], top, ALU.subtract)
                        nc.vector.scalar_tensor_tensor(r2, scol[:, bass.ds(g * GB, GB)], slope, top, ALU.mult,
                                                       ALU.subtract).then_inc(chain, 1)
                        dve.wait_ge(chain, k * 7 + 6)
                        apart(dve, k)
                        for r, col in enumerate((r1, r2)):
                            for b in range(GB):
                                last = nc.vector.tensor_scalar(diag[:, r, b * P:(b + 1) * P], m.ident[:], col[:, b:b + 1],
                                                               None, ALU.mult)
                        last.then_inc(chain, 1)
                        dve.wait_ge(rows_ready, k + 1)
                        apart(dve, k)
                        with dve.Fori(0, NB // 2) as pair:
                            t = 2 * pair
                            for u in range(2):
                                n = k * NB + t + u
                                dve.wait_ge(low_ready, n + 1)
                                apart(dve, n)
                                nc.vector.scalar_tensor_tensor(score[:, u, :], rows[:, 0, :], dcol[:, bass.ds(t + u, 1)],
                                                               score[:, u, :], ALU.add, ALU.max).then_inc(score_ready, 1)
                            for u in range(2):
                                n = k * NB + t + u
                                dve.wait_ge(exp_ready, n + 1)
                                apart(dve, n)
                                nc.vector.scalar_tensor_tensor(
                                    prob[:, u, :],
                                    mask8[:, bass.ds(g, 1), bass.ds(t + u, 1), :].rearrange("p a b n -> p (a b n)"),
                                    3.2e38 / EDGE_BYTE, prob[:, u, :], ALU.mult, ALU.min).then_inc(prob_ready, 1)
                        epilogue_recip(nc, dve, m, epi, k)
                        epilogue_elu(nc, dve, m, epi, k)
                        epilogue_variance(nc, dve, m, epi, k)

        @block.gpsimd
        def _(pool):
            bad = pool.value_load(m.bad[0:1, 0:1], min_val=0, max_val=1)
            with pool.If(bad > 0):
                pool.wait_ge(x_loaded, 16)
                nc.gpsimd.sem_inc(epi.x_ready, 1)
                with pool.Fori(0, L) as l:
                    pool.wait_ge(dve_step, l * 3 + 2)
                    apart(pool, l)
                    nc.gpsimd.partition_all_reduce(dmin_neg, dnegmax, P, RMAX).then_inc(dmin_ready, 1)
                    pool.wait_ge(hsum_ready, l + 1)
                    apart(pool, l)
                    with pool.Fori(0, G) as g:
                        k = l * G + g
                        x_g = m.x[:, bass.ds(g * GB, GB), :]
                        epilogue_empty_rows(nc, pool, m, epi, k)
                        epilogue_quotient(nc, pool, m, epi, k, x_g)
                        epilogue_norm(nc, pool, m, epi, k, x_g)

        @block.sync
        def _(sp):
            bad = sp.value_load(m.bad[0:1, 0:1], min_val=0, max_val=1)
            with sp.If(bad > 0):
                sp.dma_start(m.x[:], x.rearrange("(b p) f -> p b f", p=P)).then_inc(x_loaded, 16)
                sp.wait_ge(epi.x_ready, L * G + 1)
                sp.dma_start(out.rearrange("(b p) f -> p b f", p=P), m.x[:]).then_inc(out_done, 16)
                sp.wait_ge(out_done, 16)



def epilogue_semaphores(sem):
    e = Bag()
    e.nd_ready = sem("nd_ready")
    e.pool_step = sem("pool_step")
    e.recip_ready = sem("recip_ready")
    e.exp_min = sem("exp_min")
    e.elu_step = sem("elu_step")
    e.sum_ready = sem("sum_ready")
    e.var_ready = sem("var_ready")
    e.x_ready = sem("x_ready")
    return e


def wide(v):
    return v.unsqueeze(2).to_broadcast([P, GB, D])


def epilogue_empty_rows(nc, pool, m, e, k):
    zero = m.small[:, 0, :]
    pool.wait_ge(e.nd_ready, k + 1)
    apart(pool, k)
    nc.gpsimd.tensor_scalar(zero, m.nd[:, :, D], 0.0, None, ALU.is_equal).then_inc(e.pool_step, 1)
    pool.wait_ge(e.pool_step, k * EPI + 1)
    apart(pool, k)
    nc.gpsimd.tensor_tensor(m.t0, zero.unsqueeze(2).to_broadcast([P, GB, D + 1]),
                            m.hsum[:].unsqueeze(1).to_broadcast([P, GB, D + 1]), ALU.mult).then_inc(e.pool_step, 1)
    pool.wait_ge(e.pool_step, k * EPI + 2)
    apart(pool, k)
    nc.gpsimd.tensor_tensor(m.nd[:], m.nd[:], m.t0, ALU.add).then_inc(e.pool_step, 1)


def epilogue_quotient(nc, pool, m, e, k, x):
    recip = m.small[:, 1, :]
    h = m.t0[:, :, 0:D]
    pool.wait_ge(e.recip_ready, k + 1)
    apart(pool, k)
    nc.gpsimd.tensor_tensor(h, m.nd[:, :, 0:D], wide(recip), ALU.mult).then_inc(e.pool_step, 1)
    pool.wait_ge(e.pool_step, k * EPI + 4)
    apart(pool, k)
    nc.gpsimd.tensor_scalar(m.t1, h, 0.0, None, ALU.min).then_inc(e.pool_step, 1)
    nc.gpsimd.tensor_tensor(m.nd[:, :, 0:D], x, h, ALU.add).then_inc(e.pool_step, 1)


def epilogue_norm(nc, pool, m, e, k, x):
    s = m.small
    total, negmean, sqsum, var, rstd = (s[:, n, :] for n in range(2, 7))
    y = m.nd[:, :, 0:D]
    pool.wait_ge(e.sum_ready, k + 1)
    apart(pool, k)
    nc.gpsimd.tensor_scalar(negmean, total, -1.0 / D, 0.0, ALU.mult, ALU.add).then_inc(e.pool_step, 1)
    pool.wait_ge(e.pool_step, k * EPI + 7)
    apart(pool, k)
    nc.gpsimd.tensor_tensor(m.t1, y, wide(negmean), ALU.add).then_inc(e.pool_step, 1)
    pool.wait_ge(e.pool_step, k * EPI + 8)
    apart(pool, k)
    nc.gpsimd.tensor_tensor(m.t0[:, :, 0:D], m.t1, m.t1, ALU.mult).then_inc(e.pool_step, 1)
    pool.wait_ge(e.var_ready, k + 1)
    apart(pool, k)
    nc.gpsimd.tensor_scalar(var, sqsum, 1.0 / D, EPS, ALU.mult, ALU.add).then_inc(e.pool_step, 1)
    pool.wait_ge(e.pool_step, k * EPI + 10)
    apart(pool, k)
    nc.gpsimd.tensor_tensor(rstd, var, m.halfneg[:], ALU.pow).then_inc(e.pool_step, 1)
    pool.wait_ge(e.pool_step, k * EPI + 11)
    apart(pool, k)
    nc.gpsimd.tensor_tensor(x, m.t1, wide(rstd), ALU.mult).then_inc(e.pool_step, 1)
    pool.wait_ge(e.pool_step, k * EPI + 12)
    apart(pool, k)
    nc.gpsimd.sem_inc(e.x_ready, 1)


def epilogue_exp(nc, act, m, e, k):
    act.wait_ge(e.pool_step, k * EPI + 5)
    apart(act, k)
    nc.scalar.activation(m.t2, m.t1, ACT.Exp).then_inc(e.exp_min, 1)


def epilogue_recip(nc, dve, m, e, k):
    dve.wait_ge(e.pool_step, k * EPI + 3)
    apart(dve, k)
    nc.vector.reciprocal(m.small[:, 1, :], m.nd[:, :, D]).then_inc(e.recip_ready, 1)


def epilogue_elu(nc, dve, m, e, k):
    y = m.nd[:, :, 0:D]
    dve.wait_ge(e.exp_min, k + 1)
    apart(dve, k)
    dve.wait_ge(e.pool_step, k * EPI + 6)
    apart(dve, k)
    nc.vector.scalar_tensor_tensor(m.t1, m.t2, -1.0, m.t1, ALU.add, ALU.subtract).then_inc(e.elu_step, 1)
    dve.wait_ge(e.elu_step, k * 2 + 1)
    apart(dve, k)
    nc.vector.scalar_tensor_tensor(y, m.t1, m.pcur[:, 1:2], y, ALU.mult, ALU.add).then_inc(e.elu_step, 1)
    dve.wait_ge(e.elu_step, k * 2 + 2)
    apart(dve, k)
    nc.vector.tensor_reduce(m.small[:, 2, :], y, op=ALU.add, axis=AX_X).then_inc(e.sum_ready, 1)


def epilogue_variance(nc, dve, m, e, k):
    dve.wait_ge(e.pool_step, k * EPI + 9)
    apart(dve, k)
    nc.vector.tensor_reduce(m.small[:, 4, :], m.t0[:, :, 0:D], op=ALU.add, axis=AX_X).then_inc(e.var_ready, 1)



def fast(nc, m, x_in, adjT, ws, wTs, avecs, out):
    with ExitStack() as ctx:
        def sem(name):
            return ctx.enter_context(nc.semaphore("f_" + name))

        x_loaded = [sem(f"x_loaded{n}") for n in range(XPARTS)]
        w_loaded = sem("w_loaded")
        adj_loaded = [sem(f"adj_loaded{n}") for n in range(SRING)]
        zeroed = sem("zeroed")
        ident_ready = sem("ident_ready")
        const_ready = sem("const_ready")
        wa_in_psum = sem("wa_in_psum")
        wa_ready = sem("wa_ready")
        w_ready = sem("w_ready")
        masked = sem("masked")
        i_xT_in_psum = sem("i_xT_in_psum")
        i_xT_ready = [sem("i_xT_act"), sem("i_xT_dve")]
        i_proj_in_psum = sem("i_proj_in_psum")
        i_proj_ready = sem("i_proj_ready")
        i_srow_in_psum = sem("i_srow_in_psum")
        i_srow_ready = sem("i_srow_ready")
        xT_in_psum = sem("xT_in_psum")
        xT_ready = sem("xT_ready")
        proj_in_psum = sem("proj_in_psum")
        proj_ready = sem("proj_ready")
        square_ready = sem("square_ready")
        srow_in_psum = sem("srow_in_psum")
        srow_ready = sem("srow_ready")
        dmax_ready = sem("dmax_ready")
        dmax_in_psum = sem("dmax_in_psum")
        shift_ready = sem("shift_ready")
        dm_ready = sem("dm_ready")
        exp_ready = sem("exp_ready")
        v_ready = sem("v_ready")
        val_ready = sem("val_ready")
        high_ready = sem("high_ready")
        low_ready = sem("low_ready")
        row_step = sem("row_step")
        u_ready = sem("u_ready")
        factors_ready = sem("factors_ready")
        hpart_step = sem("hpart_step")
        hsum_in_psum = sem("hsum_in_psum")
        hsum_ready = sem("hsum_ready")
        step_act = sem("step_act")
        step_dve = sem("step_dve")
        edges_ready = sem("edges_ready")
        edges_used = sem("edges_used")
        sums_in_psum = sem("sums_in_psum")
        sums_read = sem("sums_read")
        add_step = sem("add_step")
        epi = epilogue_semaphores(sem)
        bad_ready = sem("bad_ready")
        bad_in_psum = sem("bad_in_psum")
        out_done = sem("out_done")
        dlast_ready = sem("dlast_ready")
        ROW = 5

        wT = m.sums[0:D, 0, :, :].rearrange("p b n -> p (b n)")[:, 0:3 * D].rearrange("p (n c) -> p n c", n=3)
        avec = m.sums[0:D, 1, 0, 0:2 * L].rearrange("p (l n) -> p l n", l=L)
        steps32 = m.steps[:].bitcast(U32)
        edges32 = m.edges[:].bitcast(U32)
        mask32 = m.mask[:].bitcast(U32)
        vals = m.vals[:].rearrange("p (t k n) -> p t k n", t=NB, k=4)
        xT_all = m.vals[:].bitcast(F32)[0:D, 0:N]
        dneg, dlast, dm, v, vs, u, us, q, top = (m.cols[:, n, :] for n in range(9))
        factors = m.cols[:, 5:9, :]
        hpart = m.nd[:]
        slope = m.pcur[:, 0:1]
        fsquare = m.stats[:, 0:G]
        dmax = m.stats[:, G:G + 1]
        shift = m.stats[:, G + 1:G + 2]
        edge_cases = m.stats[:, G + 2:G + 5]
        over = m.stats[:, G + 5:G + 8]
        bad = m.stats[:, G + 8:G + 9]
        block = ctx.enter_context(nc.Block())

        def values32(k, first):
            flat = m.sums[:] if first else m.stage[:].bitcast(F32)
            flat = flat.rearrange("p a b n -> p (a b n)")
            n = k % slots(first)
            return flat[:, n * VT * 2 * F:(n + 1) * VT * 2 * F].rearrange("p (t n) -> p t n", t=VT)

        def slots(first):
            return 2 if first else 4

        def dm_step(l, part):
            return 3 * l - 1 + part

        def layers(eng, layer):
            layer(0, True, False)
            with eng.Fori(1, L - 1) as l:
                layer(l, False, False)
            layer(L - 1, False, True)

        def act_tiles(c, first):
            return ACT_TILES[c % 4] if not first else ACT_TILES_FIRST[c % 4]

        def dve_steps(l, g, c, first):
            def made(first, chunks):
                return sum(act_tiles(n, first) < CT for n in range(chunks))
            here = g * made(first, NC) + made(first, c + 1)
            return here if first else (l - 1) * (G * made(False, NC)) + (G * made(True, NC) + here)

        def d_column(g, last_layer):
            return dlast if g == G - 1 and not last_layer else dneg

        @block.sync
        def _(sp):
            adj_v = adjT.rearrange("(c t p) (g i) -> g c p t i", p=P, g=G, t=CT)
            for n, l in enumerate((0, 1, 3)):
                sp.dma_start(m.wall[:, l, H_COL:], ws[n]).then_inc(w_loaded, 16)
                sp.dma_start(wT[:, n, :], wTs[n]).then_inc(w_loaded, 16)
            for l in range(L):
                sp.dma_start(avec[:, l, :], avecs[l]).then_inc(w_loaded, 16)
            x_v = x_in.rearrange("(n b p) f -> n p b f", p=P, n=XPARTS)
            for n in range(XPARTS):
                b = NB // XPARTS
                sp.dma_start(m.x[:, n * b:(n + 1) * b, :], x_v[n]).then_inc(x_loaded[n], 16)
            for n in range(G * NC):
                if n >= SRING:
                    sp.wait_ge(masked, n - SRING + 1)
                    sp.wait_ge(adj_loaded[n % SRING], 16 * (n // SRING))
                sp.dma_start(m.stage[:, n % SRING, :, :], adj_v[n // NC, n % NC]).then_inc(adj_loaded[n % SRING], 16)
            out_v = out.rearrange("(g b p) f -> g p b f", p=P, g=G)
            for g in range(G):
                sp.wait_ge(epi.x_ready, (L - 1) * G + g + 1)
                sp.dma_start(out_v[g], m.x[:, g * GB:(g + 1) * GB, :]).then_inc(out_done, 16)
            sp.wait_ge(out_done, 16 * G)

        @block.tensor
        def _(pe):
            pe.wait_ge(w_loaded, 160)
            pe.wait_ge(ident_ready, 1)
            for l in range(L):
                wt = m.ident[0:D, 0:D] if l == 2 else wT[:, (0, 1, None, 2)[l], :]
                last = nc.tensor.matmul(m.ps[0:D, 0, 2 * l:2 * l + 2], wt, avec[:, l, :], start=True, stop=True,
                                        skip_group_check=True)
            last.then_inc(wa_in_psum, 1)
            pe.wait_ge(wa_ready, 1)

            def transposes(g, bank):
                for b in range(GB):
                    last = nc.tensor.transpose(m.ps[0:D, bank, b * P:(b + 1) * P], m.x[:, g * GB + b, :], m.ident[:])
                return last

            def projections(xT, bank):
                for b in range(GB):
                    last = nc.tensor.matmul(m.ps[:, bank, b * PW:(b + 1) * PW], xT[:, b * P:(b + 1) * P], m.wcur[:],
                                            start=b == 0, stop=b == GB - 1, skip_group_check=True)
                return last

            def spread(col, bank, b):
                return nc.tensor.transpose(m.ps[:, bank, b * P:(b + 1) * P], col.to_broadcast([P, P]), m.ident[:])

            for g in range(G):
                pe.wait_ge(x_loaded[g * XPARTS // G], 16)
                transposes(g, g).then_inc(i_xT_in_psum, 1)
            pe.wait_ge(w_ready, 1)
            for g in range(G):
                pe.wait_ge(i_xT_ready[g % 2], g // 2 + 1)
                projections(xT_all[:, g * GN:(g + 1) * GN], g).then_inc(i_proj_in_psum, 1)
            pe.wait_ge(i_proj_ready, 1)
            for b in range(GB):
                last = spread(m.proj[:, b, S_COL:S_COL + 1], 0, b)
            last.then_inc(i_srow_in_psum, 1)
            pe.wait_ge(i_srow_ready, 1)
            pe.wait_ge(i_proj_ready, G)

            def spread_dmax(l):
                pe.wait_ge(dmax_ready, l + 1)
                apart(pe, l)
                spread(dmax, 7, 0).then_inc(dmax_in_psum, 1)

            def setup(j, g, step, l):
                if step == 0:
                    pe.wait_ge(epi.x_ready, j + 1)
                    apart(pe, j)
                if step < GB:
                    done = nc.tensor.transpose(m.ps[0:D, 7, step * P:(step + 1) * P], m.x[:, g * GB + step, :], m.ident[:])
                    if step == GB - 1:
                        done.then_inc(xT_in_psum, 1)
                if step == GB:
                    pe.wait_ge(xT_ready, j + 1)
                    apart(pe, j)
                    if g == 0:
                        pe.wait_ge(w_ready, l + 2)
                        apart(pe, l)
                    projections(m.xT, 7).then_inc(proj_in_psum, 1)

            def spread_next(g, b):
                block_j = (g + 1) % G * GB + b
                done = spread(m.proj[:, block_j, S_COL:S_COL + 1], 7, b)
                if b == GB - 1:
                    done.then_inc(srow_in_psum, 1)

            def layer(l, first, last_layer):
                if first:
                    spread_dmax(l)
                for g in range(G):
                    set_up = not last_layer if g >= 2 else g == 0 and not first
                    j = l * G + g - 2
                    for c in range(NC):
                        pe.wait_ge(edges_ready, (l * G + g) * NC + c + 1)
                        apart(pe, l)
                        if g == 0 and c * CT % VT == 0:
                            pe.wait_ge(low_ready, l * NV + c * CT // VT + 1)
                            apart(pe, l)
                        tiles = [(t, b) for t in range(c * CT, (c + 1) * CT) for b in range(GB)]
                        if c == 0 or c == NC - 1:
                            tiles = [(t, b) for b in range(GB) for t in range(c * CT, (c + 1) * CT)]
                        for t, b in tiles:
                            block_i = g * GB + b
                            bank = block_i % BANKS
                            if t == 0 and block_i >= BANKS:
                                pe.wait_ge(sums_read, l * NB + block_i - BANKS + 1)
                                apart(pe, l)
                            elif t == 0 and not first:
                                pe.wait_ge(sums_read, l * NB - GB + block_i % GB + 1 if block_i < GB else l * NB)
                                apart(pe, l)
                            i = slice(b * P, (b + 1) * P)
                            sums = m.ps[:, bank, 0:4 * F].rearrange("p (n f) -> p n f", n=4)
                            for part in range(2):
                                last = nc.tensor.matmul(sums[:, part::2, :], m.edges[:, c % ERING, part, t % CT, i],
                                                        vals[:, t, part::2, :], start=t == 0 and part == 0,
                                                        stop=t == NB - 1, skip_group_check=True)
                            if t == NB - 1:
                                last.then_inc(sums_in_psum, 1)
                        if c < NC - 1:
                            last.then_inc(edges_used, 1)
                        if g == 1 and c == HSUM_AT:
                            pe.wait_ge(hpart_step, l * G + G)
                            apart(pe, l)
                            pe.wait_ge(srow_ready, l * G + 1)
                            apart(pe, l)
                            if not first:
                                pe.wait_ge(proj_ready, l * G)
                                apart(pe, l)
                            for b in range(GB):
                                hs = nc.tensor.matmul(m.ps[:, 7, 256:256 + F], m.ones[:], hpart[:, b, :],
                                                      start=b == 0, stop=b == GB - 1)
                            hs.then_inc(hsum_in_psum, 1)
                        setup_at = SETUP_SOON if g == 0 or g == G - 1 else SETUP_AT
                        if set_up and c in setup_at:
                            if c == setup_at[0]:
                                pe.wait_ge(srow_ready, l * G + g)
                                apart(pe, l)
                            if c == setup_at[0] and g == 2:
                                pe.wait_ge(hsum_ready, l + 1)
                                apart(pe, l)
                            setup(j, (g - 2) % G, setup_at.index(c), l if g >= 2 else l - 1)
                        if g == G - 1 and not last_layer and c == DMAX_AT:
                            spread_dmax(l + 1)
                        if c in SPREAD_AT and not (g == G - 1 and last_layer):
                            if c == SPREAD_AT[0]:
                                if not first or g >= 1:
                                    pe.wait_ge(srow_ready, l * G + g)
                                    apart(pe, l)
                                if set_up:
                                    pe.wait_ge(proj_ready, j + 1)
                                    apart(pe, j)
                                if g == 1:
                                    pe.wait_ge(hsum_ready, l + 1)
                                    apart(pe, l)
                                if g == G - 1 or first and g == 0:
                                    pe.wait_ge(shift_ready, l + 2 if g else 1)
                                    apart(pe, l)
                            spread_next(g, SPREAD_AT.index(c))
                        if g == 0 and not first and c == LATE_AT:
                            pe.wait_ge(srow_ready, l * G + 1)
                            apart(pe, l)
                            for step in range(GB + 1):
                                setup(l * G - 1, G - 1, step, l - 1)

            layers(pe, layer)
            pe.wait_ge(bad_ready, 1)
            nc.tensor.matmul(m.ps[:, 7, 0:1], m.ones[:], bad, start=True, stop=True).then_inc(bad_in_psum, 1)

        @block.scalar
        def _(act):
            def copy_proj(g, bank):
                return nc.scalar.copy(m.proj[:, g * GB:(g + 1) * GB, 0:PW],
                                      m.ps[:, bank, 0:GB * PW].rearrange("p (b n) -> p b n", b=GB))

            def squares(g):
                return nc.scalar.activation(m.squared, m.proj[:, g * GB:(g + 1) * GB, H_COL:PW], ACT.Square,
                                            accum_out=fsquare[:, g:g + 1])

            def steps(l, g, c, first, last_layer):
                n = (l * G + g) * NC + c
                if not first or n >= TRING:
                    act.wait_ge(edges_ready, n - TRING + 1)
                    apart(act, n)
                if c == 0 and first and g == 0:
                    act.wait_ge(i_srow_ready, 1)
                elif c == 0:
                    act.wait_ge(srow_ready, l * G + g)
                    apart(act, l)
                if first and g == 0 and c == 0:
                    act.wait_ge(dm_ready, 1)
                elif not first and g == 0 and c * CT in (0, EARLY, EARLY + GB):
                    act.wait_ge(dm_ready, dm_step(l, (0, EARLY, EARLY + GB).index(c * CT)))
                    apart(act, l)
                if g == G - 1 and not last_layer and c == 0:
                    act.wait_ge(dlast_ready, l + 1)
                    apart(act, l)
                for u in range(act_tiles(c, first)):
                    t = c * CT + u
                    last = nc.scalar.activation(m.steps[:, c % TRING, u, :], m.srow[:, g % 2, :], ACT.Relu, scale=-1.0,
                                                bias=d_column(g, last_layer)[:, t:t + 1], saturate=False)
                last.then_inc(step_act, 1)

            for g in range(0, G, 2):
                act.wait_ge(i_xT_in_psum, g + 1)
                nc.scalar.copy(xT_all[:, g * GN:(g + 1) * GN], m.ps[0:D, g, :]).then_inc(i_xT_ready[0], 1)
            for g in range(G):
                act.wait_ge(i_proj_in_psum, g + 1)
                copy_proj(g, g).then_inc(i_proj_ready, 1)
            for g in range(G):
                act.wait_ge(i_proj_ready, g + 1)
                if g >= 1:
                    act.wait_ge(square_ready, g)
                squares(g).then_inc(square_ready, 1)

            def make_v(l, part, first):
                t = slice(0, NB) if first else (slice(0, EARLY), slice(EARLY, EARLY + GB), slice(EARLY + GB, NB))[part]
                act.wait_ge(dm_ready, 1 if first else dm_step(l, part))
                apart(act, l)
                nc.scalar.activation(v[:, t], dm[:, t], ACT.Exp)
                nc.scalar.activation(vs[:, t], dm[:, t], ACT.Exp, scale=slope).then_inc(exp_ready, 1)
                act.wait_ge(exp_ready, 1 if first else dm_step(l, part))
                apart(act, l)
                nc.scalar.activation(m.cols[:, 3:5, t], m.cols[:, 3:5, t], ACT.Copy, scale=UP * LOW).then_inc(v_ready, 1)

            def split(l, k, first):
                n = l * NV + k
                act.wait_ge(val_ready, n + 1)
                apart(act, n)
                if k < EARLY // VT and not first:
                    act.wait_ge(edges_used, (l * G - 1) * (NC - 1) + 2 * k + 2)
                    apart(act, l)
                nc.scalar.activation(vals[:, k * VT:(k + 1) * VT, 0:2, :].rearrange("p t k n -> p t (k n)"),
                                     values32(k, first), ACT.Copy, scale=1.0 / LOW).then_inc(high_ready, 1)

            def row_exponentials(l):
                act.wait_ge(row_step, l * ROW + 3)
                apart(act, l)
                nc.scalar.activation(u, u, ACT.Exp)
                nc.scalar.activation(us, us, ACT.Exp).then_inc(u_ready, 1)

            def evacuate(k, g):
                if not isinstance(k, int) or k >= 1:
                    act.wait_ge(epi.x_ready, k)
                    apart(act, k)
                for b in range(GB):
                    act.wait_ge(sums_in_psum, k * GB + b + 1)
                    apart(act, k)
                    nc.scalar.copy(m.sums[:, :, b, :], m.ps[:, (g * GB + b) % BANKS, 0:4 * F].rearrange(
                        "p (n f) -> p n f", n=4)).then_inc(sums_read, 1)

            def copies(l, j, g, step):
                if step == 0:
                    act.wait_ge(xT_in_psum, j + 1)
                    apart(act, j)
                    act.wait_ge(square_ready, j + G)
                    apart(act, j)
                    nc.scalar.copy(m.xT, m.ps[0:D, 7, :]).then_inc(xT_ready, 1)
                if step == 1:
                    act.wait_ge(proj_in_psum, j + 1)
                    apart(act, j)
                    if g == 0:
                        act.wait_ge(row_step, l * ROW + ROW)
                        apart(act, l)
                        act.wait_ge(hpart_step, l * G + G)
                        apart(act, l)
                    copy_proj(g, 7).then_inc(proj_ready, 1)
                    act.wait_ge(proj_ready, j + 1)
                    apart(act, j)
                    squares(g).then_inc(square_ready, 1)
                    act.wait_ge(square_ready, j + G + 1)
                    apart(act, j)

            def copy_srow(l, g):
                act.wait_ge(srow_in_psum, l * G + g + 1)
                apart(act, l)
                nc.scalar.activation(m.srow[:, (g + 1) % 2, :], m.ps[:, 7, :], ACT.Copy, scale=K).then_inc(srow_ready, 1)

            def layer(l, first, last_layer):
                for g in range(G):
                    k = l * G + g - 1
                    early = g == G - 1 and not last_layer
                    for c in range(NC):
                        steps(l, g, c, first, last_layer)
                        if c == (SROW_AT if g >= 1 else LATE_AT) and not (g == G - 1 and last_layer):
                            copy_srow(l, g)
                        if g == 0 and first:
                            if c == 0:
                                make_v(l, 0, True)
                                split(l, 0, True)
                            if c % 2 == 0 and c // 2 + 1 < NV:
                                split(l, c // 2 + 1, True)
                            if c == NC - 2:
                                row_exponentials(l)
                            continue
                        if g == 0 and c < 2:
                            split(l, EARLY // VT - 2 + c, False)
                        if c == (EVACUATE_SOON if g == 0 or early else EVACUATE_AT):
                            evacuate(k, (g - 1) % G)
                        if g == 1 and c == HCOPY_AT:
                            act.wait_ge(hsum_in_psum, l + 1)
                            apart(act, l)
                            nc.scalar.copy(m.hsum[:], m.ps[:, 7, 256:256 + F]).then_inc(hsum_ready, 1)
                        if c in COPY_AT and g == 0:
                            copies(l - 1, k - 1, G - 2, COPY_AT.index(c))
                        if c in COPY_AT and g >= 2 and not last_layer:
                            copies(l, k - 1, g - 2, COPY_AT.index(c))
                        if g == 0 and c == V_AT:
                            make_v(l, 1, False)
                        if early and c == V_AT:
                            make_v(l + 1, 0, False)
                        if early and c in SPLIT_AT:
                            split(l + 1, SPLIT_AT.index(c), False)
                        if c == (EXP_SOON if g == 0 or early else EXP_AT):
                            epilogue_exp(nc, act, m, epi, k)
                        if g == 0 and c == V_AT + 1:
                            split(l, NV - 2, False)
                        if g == 0 and c == LATE_AT:
                            for step in range(2):
                                copies(l - 1, k, G - 1, step)
                            make_v(l, 2, False)
                            split(l, NV - 1, False)
                    if g == 0 and not first:
                        row_exponentials(l)

            layers(act, layer)
            evacuate(L * G - 1, G - 1)
            epilogue_exp(nc, act, m, epi, L * G - 1)

        @block.vector
        def _(dve):
            nc.vector.memset(m.ones[:], 1.0)
            nc.vector.memset(m.halfneg[:], -0.5)
            nc.vector.memset(m.proj[:, :, PW], 1.0)
            nc.vector.memset(bad, 0.0)
            for l in range(L):
                nc.vector.memset(m.par[:, l, 0:1], SLOPES[l])
                last = nc.vector.memset(m.par[:, l, 1:2], HAS_ELU[l])
            last.then_inc(const_ready, 1)
            dve.wait_ge(const_ready, 1)

            def make_mask(n):
                if n < G * NC:
                    c = n % NC
                    dve.wait_ge(adj_loaded[n % SRING], 16 * (n // SRING + 1))
                    nc.vector.tensor_scalar(m.mask[:, n // NC, c * CT:(c + 1) * CT, :], m.stage[:, n % SRING, :, :],
                                            0, EDGE, ALU.is_gt, ALU.mult, saturate=False).then_inc(masked, 1)

            def param(col, l):
                return nc.vector.tensor_copy(m.pcur[:, col:col + 1],
                                             m.par[:, bass.ds(l, 1), col:col + 1].rearrange("p a n -> p (a n)"))

            def weights(l):
                return nc.vector.tensor_copy(m.wcur[:], m.wall[:, bass.ds(l, 1), :].rearrange("p a n -> p (a n)"))

            dve.wait_ge(ident_ready, 1)
            nc.vector.tensor_copy(m.wall[:, 2, H_COL:], m.ident[0:D, 0:D])
            param(0, 0)
            param(1, 0)
            dve.wait_ge(w_loaded, 160)
            dve.wait_ge(wa_in_psum, 1)
            for c in range(2):
                last = nc.vector.tensor_copy(m.wall[:, :, c], m.ps[0:D, 0, 0:2 * L].rearrange(
                    "p (l c) -> p l c", c=2)[:, :, c])
            last.then_inc(wa_ready, 1)
            dve.wait_ge(wa_ready, 1)
            weights(0).then_inc(w_ready, 1)
            for g in range(1, G, 2):
                dve.wait_ge(i_xT_in_psum, g + 1)
                nc.vector.tensor_copy(xT_all[:, g * GN:(g + 1) * GN], m.ps[0:D, g, :]).then_inc(i_xT_ready[1], 1)
            for n in range(AHEAD // 2):
                make_mask(n)
            dve.wait_ge(i_srow_in_psum, 1)
            nc.vector.tensor_scalar(m.srow[:, 0, :], m.ps[:, 0, :], K, None, ALU.mult).then_inc(i_srow_ready, 1)
            for n in range(AHEAD // 2, AHEAD):
                make_mask(n)

            def find_dmax(blocks):
                nc.vector.tensor_reduce(dmax, m.proj[:, 0:blocks, D_COL], op=ALU.max, axis=AX_X
                                        ).then_inc(dmax_ready, 1)

            def find_shift(l):
                dve.wait_ge(dmax_in_psum, l + 1)
                apart(dve, l)
                nc.vector.tensor_reduce(shift, m.ps[:, 7, 0:P], op=ALU.max, axis=AX_X).then_inc(shift_ready, 1)
                dve.wait_ge(shift_ready, l + 1)
                apart(dve, l)

            def subtract_shift(t):
                nc.vector.tensor_scalar(dneg[:, t], m.proj[:, t, D_COL], -K, None, ALU.mult)
                nc.vector.tensor_scalar(dm[:, t], m.proj[:, t, D_COL], shift, None, ALU.subtract).then_inc(dm_ready, 1)

            def low_part(l, k, first):
                n = l * NV + k
                dve.wait_ge(high_ready, n + 1)
                apart(dve, n)
                nc.vector.scalar_tensor_tensor(
                    vals[:, k * VT:(k + 1) * VT, 2:4, :].rearrange("p t k n -> p t (k n)"),
                    vals[:, k * VT:(k + 1) * VT, 0:2, :].rearrange("p t k n -> p t (k n)"),
                    -LOW, values32(k, first), ALU.mult, ALU.add).then_inc(low_ready, 1)

            def row_factors(l):
                nc.vector.tensor_scalar(q, m.proj[:, :, S_COL], shift, None, ALU.add).then_inc(row_step, 1)
                nc.vector.tensor_reduce(edge_cases[:, 0:1], dm, op=ALU.max, axis=AX_X)
                dve.wait_ge(row_step, l * ROW + 1)
                apart(dve, l)
                nc.vector.scalar_tensor_tensor(top, q, slope, q, ALU.mult, ALU.max).then_inc(row_step, 1)
                nc.vector.tensor_reduce(edge_cases[:, 1:2], dm, op=ALU.min, axis=AX_X)
                dve.wait_ge(row_step, l * ROW + 2)
                apart(dve, l)
                nc.vector.scalar_tensor_tensor(us, q, slope, top, ALU.mult, ALU.subtract)
                nc.vector.tensor_tensor(u, q, top, ALU.subtract).then_inc(row_step, 1)
                nc.vector.tensor_reduce(edge_cases[:, 2:3], fsquare, op=ALU.max, axis=AX_X).then_inc(row_step, 1)
                dve.wait_ge(row_step, l * ROW + 4)
                apart(dve, l)
                nc.vector.tensor_scalar(over[:, 0:1], edge_cases[:, 0:1], MAX_ABOVE, bad, ALU.is_gt, ALU.max)
                nc.vector.tensor_scalar(over[:, 1:2], edge_cases[:, 1:2], -MAX_RANGE, None, ALU.is_lt)
                nc.vector.tensor_scalar(over[:, 2:3], edge_cases[:, 2:3], MAX_SQUARE, None, ALU.is_gt
                                        ).then_inc(row_step, 1)
                dve.wait_ge(row_step, l * ROW + 5)
                apart(dve, l)
                nc.vector.tensor_reduce(bad, over, op=ALU.max, axis=AX_X)

            def low_factors(l):
                dve.wait_ge(u_ready, l + 1)
                apart(dve, l)
                nc.vector.tensor_scalar(q, u, 1.0 / LOW, None, ALU.mult)
                nc.vector.tensor_scalar(top, us, 1.0 / LOW, None, ALU.mult).then_inc(factors_ready, 1)

            def steps(l, g, c, first, last_layer):
                n = (l * G + g) * NC + c
                if c == 0 and not (first and g == 0):
                    dve.wait_ge(srow_ready, l * G + g)
                    apart(dve, l)
                if act_tiles(c, first) < CT:
                    if not first or n >= TRING:
                        dve.wait_ge(edges_ready, n - TRING + 1)
                        apart(dve, l)
                    for u in range(act_tiles(c, first), CT):
                        t = c * CT + u
                        last = nc.vector.tensor_scalar(m.steps[:, c % TRING, u, :], m.srow[:, g % 2, :],
                                                       d_column(g, last_layer)[:, t:t + 1], EDGE, ALU.is_lt, ALU.mult,
                                                       saturate=False)
                    last.then_inc(step_dve, 1)

            def edges(l, g, c, first):
                slot, tslot = c % ERING, c % TRING
                back = g * NC + c - ERING
                if back % NC == NC - 1 and (back >= 0 or not first):
                    dve.wait_ge(sums_in_psum, l * NB + (back // NC + 1) * GB)
                    apart(dve, l)
                elif back >= 0 or not first:
                    dve.wait_ge(edges_used, (l * G + back // NC) * (NC - 1) + back % NC + 1)
                    apart(dve, l)
                dve.wait_ge(step_act, (l * G + g) * NC + c + 1)
                apart(dve, l)
                if not first or dve_steps(l, g, c, first) > 0:
                    dve.wait_ge(step_dve, dve_steps(l, g, c, first))
                    apart(dve, l)
                t = slice(c * CT, (c + 1) * CT)
                nc.vector.scalar_tensor_tensor(edges32[:, slot, 0, :, :], steps32[:, tslot, :, :], EDGE_WORD,
                                               mask32[:, g, t, :], ALU.bitwise_xor, ALU.bitwise_and)
                nc.vector.tensor_tensor(edges32[:, slot, 1, :, :], steps32[:, tslot, :, :], mask32[:, g, t, :],
                                        ALU.bitwise_and).then_inc(edges_ready, 1)

            def layer(l, first, last_layer):
                if first:
                    dve.wait_ge(i_proj_ready, G)
                    find_dmax(NB)
                    dve.wait_ge(i_srow_ready, 1)
                    find_shift(l)
                    subtract_shift(slice(0, NB))
                    dve.wait_ge(dm_ready, 1)
                    steps(0, 0, 0, True, False)
                    low_part(l, 0, True)
                for g in range(G):
                    k = l * G + g - 1
                    early = g == G - 1 and not last_layer
                    for c in range(NC):
                        if first:
                            make_mask(g * NC + c + AHEAD)
                        late = g == 0 and not first and c == LATE_AT
                        if late:
                            edges(l, g, c, first)
                            dve.wait_ge(proj_ready, l * G)
                            apart(dve, l)
                            subtract_shift(slice(EARLY + GB, NB))
                            dve.wait_ge(dm_ready, dm_step(l, 2))
                            apart(dve, l)
                        if g == G - 2 and c == NC - 2 and not last_layer:
                            dve.wait_ge(dlast_ready, l + 1)
                            apart(dve, l)
                        if c < NC - 1:
                            steps(l, g, c + 1, first, last_layer)
                        elif g < G - 1:
                            steps(l, g + 1, 0, first, last_layer)
                        elif not last_layer:
                            dve.wait_ge(dm_ready, dm_step(l + 1, 0))
                            apart(dve, l)
                            steps(l + 1, 0, 0, False, False)
                        if not late:
                            edges(l, g, c, first)
                        if g == 0 and first:
                            if c % 2 == 1 and c < NC - 1:
                                low_part(l, (c + 1) // 2, True)
                            if c == 3:
                                dve.wait_ge(square_ready, G)
                                row_factors(l)
                            if c == 12:
                                weights(l + 1).then_inc(w_ready, 1)
                        if g == 0 and not first:
                            if c < EARLY // VT - len(LOWS_AT):
                                low_part(l, len(LOWS_AT) + c, False)
                            if c == SHIFT_AT:
                                dve.wait_ge(proj_ready, l * G - 1)
                                apart(dve, l)
                                subtract_shift(slice(EARLY, EARLY + GB))
                                dve.wait_ge(dm_ready, dm_step(l, 1))
                                apart(dve, l)
                            if c == LOW6_AT:
                                low_part(l, NV - 2, False)
                                param(1, l)
                            if c == LATE_AT:
                                low_part(l, NV - 1, False)
                            if c == NC - 1:
                                dve.wait_ge(square_ready, l * G + G)
                                apart(dve, l)
                                row_factors(l)
                                if not last_layer:
                                    weights(l + 1).then_inc(w_ready, 1)
                        if g == 1 and c == 0:
                            low_factors(l)
                        if g == G - 3 and c == 0 and not last_layer:
                            nc.vector.tensor_copy(dlast, dneg).then_inc(dlast_ready, 1)
                        if early:
                            if c == DMAX_AT - 1:
                                dve.wait_ge(proj_ready, l * G + G - 2)
                                apart(dve, l)
                                param(0, l + 1)
                                find_dmax(EARLY)
                            if c == DMAX_AT + 1:
                                find_shift(l + 1)
                                subtract_shift(slice(0, EARLY))
                            if c in LOWS_AT:
                                low_part(l + 1, LOWS_AT.index(c), False)
                        if not first or g >= 1:
                            if c == (RECIP_SOON if g == 0 or early else RECIP_AT):
                                epilogue_recip(nc, dve, m, epi, k)
                            if c == (ELU_SOON if g == 0 or early else ELU_AT):
                                epilogue_elu(nc, dve, m, epi, k)
                            if c == (VARIANCE_SOON if g == 0 or early else VARIANCE_AT):
                                epilogue_variance(nc, dve, m, epi, k)

            layers(dve, layer)
            epilogue_recip(nc, dve, m, epi, L * G - 1)
            epilogue_elu(nc, dve, m, epi, L * G - 1)
            epilogue_variance(nc, dve, m, epi, L * G - 1)
            dve.wait_ge(row_step, L * ROW)
            nc.vector.tensor_copy(over[:, 0:1], bad).then_inc(bad_ready, 1)
            dve.wait_ge(bad_in_psum, 1)
            nc.vector.tensor_scalar(m.bad[:], m.ps[:, 7, 0:1], 0.5, None, ALU.is_gt).then_inc(bad_ready, 1)
            dve.wait_ge(bad_ready, 2)

        @block.gpsimd
        def _(pool):
            nc.gpsimd.memset(m.ident[:], 0.0).then_inc(zeroed, 1)
            pool.wait_ge(zeroed, 1)
            nc.gpsimd.affine_select(out=m.ident[:], in_=m.ident[:], compare_op=ALU.not_equal, fill=1.0, base=0,
                                    pattern=[[-1, P]], channel_multiplier=1).then_inc(ident_ready, 1)
            pool.wait_ge(const_ready, 1)

            def values(l, k, first):
                n = l * NV + k
                t = slice(k * VT, (k + 1) * VT)
                part = 0 if k < EARLY // VT else k - EARLY // VT + 1
                pool.wait_ge(v_ready, 1 if first else dm_step(l, part))
                apart(pool, l)
                if k >= slots(first) or not first:
                    pool.wait_ge(low_ready, n - slots(first) + 1)
                    apart(pool, n)
                for c, col in enumerate((v, vs)):
                    last = nc.gpsimd.tensor_tensor(values32(k, first)[:, :, c * F:(c + 1) * F], m.proj[:, t, H_COL:],
                                                   col[:, t].unsqueeze(2).to_broadcast([P, VT, F]), ALU.mult)
                last.then_inc(val_ready, 1)

            def sum_features(l):
                for g in range(1, G):
                    a = m.proj[:, 0:GB, H_COL:] if g == 1 else hpart
                    if g >= 2:
                        pool.wait_ge(hpart_step, l * G + g - 1)
                        apart(pool, l)
                    nc.gpsimd.tensor_tensor(hpart, a, m.proj[:, g * GB:(g + 1) * GB, H_COL:], ALU.add
                                            ).then_inc(hpart_step, 1 if g < G - 1 else 2)

            def add_sums(k, g):
                pool.wait_ge(sums_read, (k + 1) * GB)
                apart(pool, k)
                high, low = m.sums[:, 0:2, :, :], m.sums[:, 2:4, :, :]
                nc.gpsimd.tensor_tensor(m.sums[:], m.sums[:], factors[:, :, g * GB:(g + 1) * GB].unsqueeze(3).to_broadcast(
                    [P, 4, GB, F]), ALU.mult).then_inc(add_step, 1)
                pool.wait_ge(add_step, k * 2 + 1)
                apart(pool, k)
                nc.gpsimd.tensor_tensor(high, high, low, ALU.add).then_inc(add_step, 1)
                pool.wait_ge(add_step, k * 2 + 2)
                apart(pool, k)
                nc.gpsimd.tensor_tensor(m.nd[:], m.sums[:, 0, :, :], m.sums[:, 1, :, :], ALU.add
                                        ).then_inc(epi.nd_ready, 1)

            def layer(l, first, last_layer):
                for g in range(G):
                    k = l * G + g - 1
                    early = g == G - 1 and not last_layer
                    if g == 0 and first:
                        for n in range(NV):
                            values(l, n, True)
                        sum_features(l)
                        continue
                    x = m.x[:, (g - 1) % G * GB:((g - 1) % G + 1) * GB, :]
                    if g == 1:
                        pool.wait_ge(factors_ready, l + 1)
                        apart(pool, l)
                        pool.wait_ge(hsum_ready, l + 1)
                        apart(pool, l)
                    add_sums(k, (g - 1) % G)
                    epilogue_empty_rows(nc, pool, m, epi, k)
                    epilogue_quotient(nc, pool, m, epi, k, x)
                    if g == 0:
                        values(l, NV - 2, False)
                    if early:
                        if first:
                            pool.wait_ge(masked, G * NC)
                        for n in range(3):
                            values(l + 1, n, False)
                    epilogue_norm(nc, pool, m, epi, k, x)
                    if g == 0:
                        values(l, NV - 1, False)
                        sum_features(l)
                    if early:
                        for n in range(3, EARLY // VT):
                            values(l + 1, n, False)

            layers(pool, layer)
            k = L * G - 1
            x = m.x[:, NB - GB:, :]
            add_sums(k, G - 1)
            epilogue_empty_rows(nc, pool, m, epi, k)
            epilogue_quotient(nc, pool, m, epi, k, x)
            epilogue_norm(nc, pool, m, epi, k, x)


def gat_stack(nc, x, adjT, W0, W1, W3, WT0, WT1, WT3, a0, a1, a2, a3, out):
    with ExitStack() as ctx:
        m = place(nc, ctx)
        fast(nc, m, x, adjT, (W0, W1, W3), (WT0, WT1, WT3), (a0, a1, a2, a3), out)
        general(nc, m, x, out)


def kernel(x, adj, L0_gnn_W, L0_gnn_a, L1_gnn_W, L1_gnn_a, L2_gnn_a, L3_gnn_W, L3_gnn_a):
    import numpy as _np
    import concourse.bacc as _bacc
    from concourse import mybir as _mybir
    from concourse.bass_utils import run_bass_kernel_spmd as _run

    nc = _bacc.Bacc("TRN2", target_bir_lowering=False, num_devices=1)
    given = {"x": x, "adjT": _np.asarray(adj).T, "W0": L0_gnn_W, "W1": L1_gnn_W, "W3": L3_gnn_W,
             "WT0": _np.asarray(L0_gnn_W).T, "WT1": _np.asarray(L1_gnn_W).T, "WT3": _np.asarray(L3_gnn_W).T,
             "a0": _np.asarray(L0_gnn_a).reshape(2, 64).T, "a1": _np.asarray(L1_gnn_a).reshape(2, 64).T,
             "a2": _np.asarray(L2_gnn_a).reshape(2, 64).T, "a3": _np.asarray(L3_gnn_a).reshape(2, 64).T}
    arrays, args = {}, []
    for name, value in given.items():
        a = _np.ascontiguousarray(value)
        arrays[f"in_{name}_dram"] = a
        args.append(nc.dram_tensor(f"in_{name}_dram", a.shape, _mybir.dt.from_np(a.dtype), kind="ExternalInput").ap())
    out = nc.dram_tensor("out_0_dram", (4096, 64), _mybir.dt.float32, kind="ExternalOutput").ap()
    gat_stack(nc, *args, out)
    r = _run(nc, [arrays], core_ids=[0])
    return r.results[0]["out_0_dram"]
```
